# Optimizing a Trainium2 kernel written in Bass

```python
import numpy as np
import jax
import jax.numpy as jnp

def _softmax(x, axis=-1):
    return jax.nn.softmax(x, axis=axis)

def _gelu(x):
    return jax.nn.gelu(x, approximate=True)

def _silu(x):
    return jax.nn.silu(x)

def _sigmoid(x):
    return jax.nn.sigmoid(x)

def _layernorm(x, axis=-1, eps=1e-05):
    m = jnp.mean(x, axis=axis, keepdims=True)
    v = jnp.var(x, axis=axis, keepdims=True)
    return (x - m) / jnp.sqrt(v + eps)

def _scatter_add(tgt, idx, src, axis=0):
    return tgt.at[idx].add(src)

def _segment_sum(src, seg, n):
    return jax.ops.segment_sum(src, seg, n)
kernel_name = 'mk_gnn_preln_d2_gnn_r8_14eea4'

def setup_inputs(seed: int=0):
    np.random.seed(seed)
    _w = jnp.asarray

    def _rec_inputs():
        import jax
        import jax.numpy as jnp
        _gk = jax.random.key(seed)
        x = -0.0005121 + 1.001 * jax.random.normal(jax.random.fold_in(_gk, 1), (12500, 32), jnp.float32)
        src = jax.random.randint(jax.random.fold_in(_gk, 2), (400000,), 0, 12500, jnp.int32)
        dst = jax.random.randint(jax.random.fold_in(_gk, 3), (400000,), 0, 12500, jnp.int32)
        _o = jnp.argsort(dst, stable=True)
        src = src[_o]
        dst = dst[_o]
        edge_attr_32 = 0.000216709 + 1.00012 * jax.random.normal(jax.random.fold_in(_gk, 11), (400000, 32), jnp.float32)
        edge_attr_4 = 0.000714719 + 1.00021 * jax.random.normal(jax.random.fold_in(_gk, 12), (400000, 4), jnp.float32)
        edge_weight = 0.000452788 + 0.999756 * jax.random.normal(jax.random.fold_in(_gk, 14), (400000,), jnp.float32)
        return (x, src, dst, edge_attr_32, edge_attr_4, edge_weight)
    x, src, dst, edge_attr_32, edge_attr_4, edge_weight = _rec_inputs()

    def _L0_gnn_setup():
        import jax, jax.numpy as jnp
        import numpy as np
        N_NODES = 12500
        N_EDGES = 200000
        D_FEAT = 32
        key = jax.random.key(seed)
        k1, k2, k3 = jax.random.split(key, 3)
        x = jax.random.normal(k1, (N_NODES, D_FEAT), dtype=jnp.float32)
        a = jax.random.randint(k2, (2, N_EDGES), 0, N_NODES, dtype=jnp.int64)
        e = jax.random.normal(k3, (N_EDGES,), dtype=jnp.float32)
        return {'x': x, 'a': a, 'e': e}
    _L0_gnn_all = _L0_gnn_setup()
    _L0_gnn_in = {k: v for k, v in _L0_gnn_all.items() if k in ()}
    del _L0_gnn_all

    def _L1_gnn_setup():
        import jax, jax.numpy as jnp
        import numpy as np
        MUL = 8
        N_NODES = 12500
        N_EDGES = 100000
        EDGE_DIM = 32
        MLP_DIM = 64
        W_NUMEL = 4 * MUL * MUL
        ALPHA = 0.25
        C110 = 1.0 / np.sqrt(3.0)
        SI_SCALE = 1.0 / np.sqrt(MUL)
        key = jax.random.key(seed)
        ks = jax.random.split(key, 10)
        node_attr = jax.random.normal(ks[0], (N_NODES, 4 * MUL), dtype=jnp.float32)
        edge_index = jax.random.randint(ks[1], (2, N_EDGES), 0, N_NODES, dtype=jnp.int64)
        edge_sh = jax.random.normal(ks[2], (N_EDGES, 4), dtype=jnp.float32)
        edge_feat = jax.random.normal(ks[3], (N_EDGES, EDGE_DIM), dtype=jnp.float32)
        W1 = jax.random.normal(ks[4], (EDGE_DIM, MLP_DIM), dtype=jnp.float32) / np.sqrt(EDGE_DIM)
        b1 = jnp.zeros((MLP_DIM,), dtype=jnp.float32)
        W2 = jax.random.normal(ks[5], (MLP_DIM, W_NUMEL), dtype=jnp.float32) / np.sqrt(MLP_DIM)
        b2 = jnp.zeros((W_NUMEL,), dtype=jnp.float32)
        si_w0 = jax.random.normal(ks[6], (MUL, MUL), dtype=jnp.float32)
        si_w1 = jax.random.normal(ks[7], (MUL, MUL), dtype=jnp.float32)
        return {'node_attr': node_attr, 'edge_index': edge_index, 'edge_sh': edge_sh, 'edge_feat': edge_feat, 'W1': W1, 'b1': b1, 'W2': W2, 'b2': b2, 'si_w0': si_w0, 'si_w1': si_w1}
    _L1_gnn_all = _L1_gnn_setup()
    _L1_gnn_in = {k: v for k, v in _L1_gnn_all.items() if k in ('W1', 'b1', 'W2', 'b2', 'si_w0', 'si_w1')}
    del _L1_gnn_all
    return {'x': x, 'src': src, 'dst': dst, 'edge_attr_32': edge_attr_32, 'edge_attr_4': edge_attr_4, 'edge_weight': edge_weight, 'L1_gnn_W1': _L1_gnn_in['W1'], 'L1_gnn_b1': _L1_gnn_in['b1'], 'L1_gnn_W2': _L1_gnn_in['W2'], 'L1_gnn_b2': _L1_gnn_in['b2'], 'L1_gnn_si_w0': _L1_gnn_in['si_w0'], 'L1_gnn_si_w1': _L1_gnn_in['si_w1']}

def reference(x, src, dst, edge_attr_32, edge_attr_4, edge_weight, L1_gnn_W1, L1_gnn_b1, L1_gnn_W2, L1_gnn_b2, L1_gnn_si_w0, L1_gnn_si_w1):
    import jax
    import jax.numpy as jnp

    def _L0_gnn_ref(x, a, e):
        import jax, jax.numpy as jnp
        import numpy as np
        N_NODES = 12500
        N_EDGES = 200000
        D_FEAT = 32
        src = a[0]
        tgt = a[1]
        msgs = x[src] * e[:, None]
        out = jax.ops.segment_sum(msgs, tgt, num_segments=x.shape[0])
        return out

    def _L1_gnn_ref(node_attr, edge_index, edge_sh, edge_feat, W1, b1, W2, b2, si_w0, si_w1):
        import jax, jax.numpy as jnp
        import numpy as np
        MUL = 8
        N_NODES = 12500
        N_EDGES = 100000
        EDGE_DIM = 32
        MLP_DIM = 64
        W_NUMEL = 4 * MUL * MUL
        ALPHA = 0.25
        C110 = 1.0 / np.sqrt(3.0)
        SI_SCALE = 1.0 / np.sqrt(MUL)
        n = node_attr.shape[0]
        e = edge_sh.shape[0]
        h = jax.nn.relu(edge_feat @ W1 + b1)
        w = (h @ W2 + b2).reshape(e, 4, MUL, MUL)
        w_000, w_011, w_101, w_110 = (w[:, 0], w[:, 1], w[:, 2], w[:, 3])
        s = node_attr[:, :MUL]
        v = node_attr[:, MUL:].reshape(n, MUL, 3)
        src, dst = (edge_index[0], edge_index[1])
        s_e = s[src]
        v_e = v[src]
        sh0 = edge_sh[:, 0]
        sh1 = edge_sh[:, 1:4]
        m0 = ALPHA * (jnp.einsum('ei,eio->eo', s_e * sh0[:, None], w_000) + C110 * jnp.einsum('eim,em,eio->eo', v_e, sh1, w_110))
        m1 = ALPHA * (jnp.einsum('ei,em,eio->eom', s_e, sh1, w_011) + jnp.einsum('eim,eio->eom', v_e * sh0[:, None, None], w_101))
        out0 = jax.ops.segment_sum(m0, dst, num_segments=n)
        out1 = jax.ops.segment_sum(m1.reshape(e, MUL * 3), dst, num_segments=n).reshape(n, MUL, 3)
        out0 = out0 + SI_SCALE * (s @ si_w0)
        out1 = out1 + SI_SCALE * jnp.einsum('nim,io->nom', v, si_w1)
        return jnp.concatenate([out0, out1.reshape(n, MUL * 3)], axis=-1)
    edge_index = jnp.stack([src, dst])
    h = jnp.maximum(_layernorm(x, axis=-1), 0.0)
    x = x + _L0_gnn_ref(h, edge_index, edge_weight)
    h = jnp.maximum(_layernorm(x, axis=-1), 0.0)
    x = x + _L1_gnn_ref(h, edge_index, edge_attr_4, edge_attr_32, L1_gnn_W1, L1_gnn_b1, L1_gnn_W2, L1_gnn_b2, L1_gnn_si_w0, L1_gnn_si_w1)
    return x

_drawn_inputs = setup_inputs


def setup_inputs(seed=0):
    import zlib

    import numpy as np

    out = dict(_drawn_inputs(seed))
    spreads = {'L1_gnn_b1': (0.0, 0.1), 'L1_gnn_b2': (0.0, 0.1)}
    factors = {}
    for name, (base, spread) in spreads.items():
        noise = np.random.default_rng([zlib.crc32(name.encode()), seed]).standard_normal(out[name].shape)
        drawn = base * np.exp(spread * noise) if base else spread * noise
        out[name] = jnp.asarray(drawn.astype(out[name].dtype))
    for name, factor in factors.items():
        out[name] = (out[name] * factor).astype(out[name].dtype)
    return out
```

```python
from contextlib import ExitStack

import concourse.bass as bass
from concourse import mybir

P = 128
G = 5
SUP = G * P
HALF = SUP // 2
WIN = 64
RING = 4
MUL = 8
D = 4 * MUL
HID = 64
BLK = MUL * MUL
WN = 4 * BLK
HV = (MUL // 2) * 3 * MUL
JG = 4
EPS = 1e-5

F32 = mybir.dt.float32
I32 = mybir.dt.int32
ALU = mybir.AluOpType
ACT = mybir.ActivationFunctionType
AX = mybir.AxisListType.X


def largest_divisor(n, most):
    return max(k for k in range(1, most + 1) if n % k == 0)


def gnn_two_layers(nc, x, src_t, dst_flat, dst_t, ew_t, sh_t, ft, w1_2, b1_2, w2_aug, si_mat, iota,
                   ident, sel, out):
    N = x.shape[0]
    S = src_t.shape[0]
    T = S * G
    NP = largest_divisor(N, 125)
    J = N // NP
    GR = J // JG
    GU = largest_divisor(GR, 5)
    SPP = largest_divisor(S, 125)
    SK = S // SPP
    FULL = S // RING
    NWIN = -(-N // WIN)
    AW = NWIN * WIN + WIN
    assert J % JG == 0 and FULL >= 2

    def uses(r):
        return FULL + (1 if r < S % RING else 0)

    with ExitStack() as ctx:
        def sb(name, shape, dt=F32):
            return ctx.enter_context(nc.sbuf_tensor(name, shape, dt))

        def psum(name, shape):
            return ctx.enter_context(nc.psum_tensor(name, shape, F32))

        def sem(name):
            return ctx.enter_context(nc.semaphore(name))

        def sems(name):
            return [sem(f"{name}{r}") for r in range(RING)]

        h0_dram = nc.dram_tensor("h0_table", [N, D], F32).ap()
        h1_dram = nc.dram_tensor("h1_table", [N, D], F32).ap()
        base_dram = nc.dram_tensor("base_table", [S], I32).ap()
        span_dram = nc.dram_tensor("span_table", [S], I32).ap()

        w_ps = psum("w_ps", [P, 2, 3, 512])
        hp_ps = psum("hp_ps", [P, 512])
        sc_ps = psum("sc_ps", [P, 512])
        wts_ps = [w_ps[:, q].rearrange("p k n -> p (k n)")[:, 0:G * WN].rearrange("p (g n) -> p g n", g=G)
                  for q in range(2)]
        sums_ps = sc_ps[:, 0:2 * WIN].rearrange("p (k n) -> p k n", k=2)
        fold_ps = w_ps[:].rearrange("p q k n -> p (q k) n")

        acc = sb("acc", [P, 2, AW])
        x_sb = sb("x_sb", [NP, J * D])
        big = sb("big", [P, max(J * D, SK * SUP)])
        st_sum, st_neg, st_var = (sb(n, [NP, J]) for n in ("st_sum", "st_neg", "st_var"))
        st_eps, st_std, st_inv = (sb(n, [NP, J]) for n in ("st_eps", "st_std", "st_inv"))
        stage_flat = sb("stage", [P, max(GU * 2 * JG * NP, J * D)])
        stage = stage_flat[:, 0:GU * 2 * JG * NP].rearrange("p (k b j n) -> p k b j n", k=GU, b=2, j=JG)
        feat = sb("feat", [NP, GU, JG * D])
        rel_sb = sb("rel_sb", [P, T])
        base_row, span_row = sb("base_row", [1, S], I32), sb("span_row", [1, S], I32)
        span_max = sb("span_max", [1, 1], I32)
        base_bc = sb("base_bc", [P, S], I32)
        least, most = sb("least", [SPP, SK]), sb("most", [SPP, SK])
        least_i, span_i = sb("least_i", [SPP, SK], I32), sb("span_i", [SPP, SK], I32)
        iota_sb = sb("iota_sb", [P, WIN])
        wide_dst, wide_near = sb("wide_dst", [P, G]), sb("wide_near", [P, G])
        id_sb = sb("id_sb", [P, P])
        sel_sb = sb("sel_sb", [P, 3, D])
        w1_sb = sb("w1_sb", [P, P])
        b1_sb = sb("b1_sb", [P, 1])
        w2_sb = sb("w2_sb", [P, WN])
        si_raw, si_sb = sb("si_raw", [JG * D, JG * D]), sb("si_sb", [JG * D, JG * D])
        idx = sb("idx", [P, RING, G], I32)
        ew_sb = sb("ew_sb", [P, RING, G])
        z = sb("z", [P, RING, G, D])
        onehot = sb("onehot", [P, RING, G, WIN])
        ft_sb = sb("ft_sb", [P, RING, HALF])
        sh_sb = sb("sh_sb", [P, RING, G, 4])
        hid = sb("hid", [P, 2, SUP])
        coef = sb("coef", [P, G, MUL + D])
        vsh = sb("vsh", [P, G, MUL, 3])
        p011 = sb("p011", [P, G, MUL, MUL])
        t011 = sb("t011", [P, G, MUL])
        p101 = sb("p101", [P, G, MUL, 3 * MUL])
        prod1 = sb("prod1", [P, 2, G, 2 * MUL, MUL])
        prod2 = sb("prod2", [P, 2, G, P])

        x_in, dst_in, dstt_in, const_in = (
            sem(n) for n in ("x_in", "dst_in", "dstt_in", "const_in"))
        reduced, table_ready, tab_out, tab_in, rel_ready = (
            sem(n) for n in ("reduced", "table_ready", "tab_out", "tab_in", "rel_ready"))
        cleared, ones_set, pads_set = sem("cleared"), sem("ones_set"), sem("pads_set")
        norm_step, var_ready, std_ready, h_ready, h_out = (
            sem(n) for n in ("norm_step", "var_ready", "std_ready", "h_ready", "h_out"))
        staged0, folded0, added0 = sem("staged0"), sem("folded0"), sem("added0")
        staged1, folded1, added1, res_out = sem("staged1"), sem("folded1"), sem("added1"), sem("res_out")
        si_scaled, feat_staged, turned, turned_copied, si_done, si_added = (
            sem(n) for n in ("si_scaled", "feat_staged", "turned", "turned_copied", "si_done", "si_added"))
        idx0_in, z0_in, ew_in = sems("idx0_in"), sems("z0_in"), sems("ew_in")
        msg0_ready, sum0_ready, acc0_done = sem("msg0_ready"), sem("sum0_ready"), sem("acc0_done")
        idx1_in, z1_in, sh_in, ft_in = sems("idx1_in"), sems("z1_in"), sems("sh_in"), sems("ft_in")
        hidpre_ready, hid_ready, wts_ready, wts_used = (
            sem(n) for n in ("hidpre_ready", "hid_ready", "wts_ready", "wts_used"))
        prod_step, msg1_ready, sum1_ready, acc1_done = (
            sem(n) for n in ("prod_step", "msg1_ready", "sum1_ready", "acc1_done"))

        def supertiles(eng, body, lag=0):
            for s in range(RING):
                body(0, s, s)
            with eng.Fori(1, FULL) as b:
                for r in range(RING):
                    body(b, r, None)
            for s in range(FULL * RING, S + lag):
                body(s // RING, s % RING, s)

        def groups(eng, body):
            for k in range(GU):
                body(k, k, True)
            if GR > GU:
                with eng.Fori(1, GR // GU) as g:
                    for k in range(GU):
                        body(g * GU + k, k, False)

        span_ready = sem("span_ready")
        wide_free, wide_in, wide_z = ([sem(f"{n}{layer}") for layer in (0, 1)] for n in ("wide_free", "wide_in", "wide_z"))
        wide_step, wide_hot, wide_sum = ([sem(f"{n}{layer}") for layer in (0, 1)] for n in ("wide_step", "wide_hot", "wide_sum"))
        wide_added = [sem("wide_added0"), sem("wide_added1")]

        def if_wide(eng):
            eng.wait_ge(span_ready, 1)
            return eng.If(eng.value_load(span_max[0:1, 0:1], min_val=0, max_val=N - 1) >= WIN)

        block = ctx.enter_context(nc.Block())

        @block.sync
        def _(sp):
            sp.dma_start(big[0:SPP, 0:SK * SUP].bitcast(I32),
                         dst_flat.rearrange("(p e) -> p e", p=SPP)).then_inc(dst_in, 16)
            sp.dma_start(x_sb[:], x.rearrange("(p j) d -> p (j d)", p=NP)).then_inc(x_in, 16)
            sp.dma_start(rel_sb[:].bitcast(I32), dst_t).then_inc(dstt_in, 16)
            for to, of in ((iota_sb, iota), (id_sb, ident), (sel_sb, sel), (w1_sb, w1_2), (b1_sb, b1_2),
                           (w2_sb, w2_aug), (si_raw, si_mat)):
                sp.dma_start(to[:], of).then_inc(const_in, 16)
            sp.wait_ge(table_ready, 2)
            sp.dma_start(base_dram.rearrange("(p k) -> p k", p=SPP), least_i[:]).then_inc(tab_out, 16)
            sp.dma_start(span_dram.rearrange("(p k) -> p k", p=SPP), span_i[:]).then_inc(tab_out, 16)
            sp.wait_ge(tab_out, 32)
            sp.dma_start(base_row[:], base_dram.rearrange("(a s) -> a s", a=1)).then_inc(tab_in, 16)
            sp.dma_start(span_row[:], span_dram.rearrange("(a s) -> a s", a=1)).then_inc(tab_in, 16)
            sp.dma_start(base_bc[:], base_dram.rearrange("(a s) -> a s", a=1).to_broadcast([P, S])
                         ).then_inc(tab_in, 16)
            sp.wait_ge(h_ready, 1)
            sp.dma_start(h0_dram.rearrange("(p j) d -> p (j d)", p=NP), big[0:NP, 0:J * D]).then_inc(h_out, 16)

            def load0(b, r, s):
                n = b * RING + r
                if s is None or s >= RING:
                    sp.wait_ge(z0_in[r], b * 16 * G)
                sp.dma_start(idx[:, r, :], src_t[n]).then_inc(idx0_in[r], 16)
                if s is None or s >= RING:
                    sp.wait_ge(msg0_ready, n - RING + 1)
                sp.dma_start(ew_sb[:, r, :], ew_t[n]).then_inc(ew_in[r], 16)
            supertiles(sp, load0)

            def wide_loads(layer, loads):
                with if_wide(sp):
                    with sp.Fori(0, S) as n:
                        sp.wait_ge(wide_free[layer], n + 1)
                        for to, of in loads:
                            sp.dma_start(to, of[n]).then_inc(wide_in[layer], 16)
                    sp.wait_ge(wide_free[layer], S + 1)
            wide_loads(0, [(idx[:, 0, :], src_t), (ew_sb[:, 0, :], ew_t)])

            sp.wait_ge(h_ready, 2)
            sp.dma_start(h1_dram.rearrange("(p j) d -> p (j d)", p=NP), big[0:NP, 0:J * D]).then_inc(h_out, 16)

            def load1(b, r, s):
                n = b * RING + r
                if s is not None and s < RING:
                    sp.wait_ge(z0_in[r], uses(r) * 16 * G)
                else:
                    sp.wait_ge(z1_in[r], b * 16 * G)
                sp.dma_start(idx[:, r, :], src_t[n]).then_inc(idx1_in[r], 16)
                if s is None or s >= RING:
                    sp.wait_ge(hidpre_ready, n - RING + 1)
                sp.dma_start(ft_sb[0:2 * D, r, :], ft[n]).then_inc(ft_in[r], 16)
                if s is None or s >= RING:
                    sp.wait_ge(msg1_ready, n - RING + 1)
                sp.dma_start(sh_sb[:, r].rearrange("p g c -> p (g c)"), sh_t[n]).then_inc(sh_in[r], 16)
            supertiles(sp, load1)
            wide_loads(1, [(idx[:, 0, :], src_t), (ft_sb[0:2 * D, 0, :], ft), (sh_sb[:, 0].rearrange("p g c -> p (g c)"), sh_t)])

            sp.wait_ge(added1, GR)
            sp.dma_start(out.rearrange("(p j) d -> p (j d)", p=NP), x_sb[:]).then_inc(res_out, 16)
            sp.wait_ge(res_out, 16)

        @block.gpsimd
        def _(pool):
            pool.memset(acc[:, 0, :], 0.0).then_inc(cleared, 1)
            pool.memset(acc[:, 1, :], 0.0).then_inc(cleared, 1)
            pool.wait_ge(cleared, 2)
            pool.memset(ft_sb[2 * D:], 0.0).then_inc(cleared, 1)
            pool.wait_ge(cleared, 3)
            pool.memset(hid[HID:], 0.0).then_inc(cleared, 1)
            pool.wait_ge(cleared, 4)
            pool.memset(hid[HID:HID + 1], 1.0).then_inc(ones_set, 1)
            pool.wait_ge(ones_set, 1)
            pool.memset(prod2[:, :, :, HV + 3 * MUL:P], 0.0).then_inc(pads_set, 1)

            def gathers(table, idx_in, z_in, used):
                def gather(b, r, s):
                    n = b * RING + r
                    pool.wait_ge(idx_in[r], (b + 1) * 16)
                    if s is None or s >= RING:
                        pool.nop(nofuse=True)
                        pool.wait_ge(used, n - RING + 1)
                    pool.nop(nofuse=True)
                    for u in range(G):
                        pool.indirect_dma_start(
                            z[:, r, u, :], None, table,
                            bass.IndirectOffsetOnAxis(ap=idx[:, r, u:u + 1], axis=0)).then_inc(z_in[r], 16)
                return gather

            pool.wait_ge(pads_set, 1)
            pool.nop(nofuse=True)
            pool.wait_ge(h_out, 16)
            pool.nop(nofuse=True)
            supertiles(pool, gathers(h0_dram, idx0_in, z0_in, sum0_ready))

            def wide_gathers(layer, table, loads):
                with if_wide(pool):
                    with pool.Fori(0, S) as n:
                        pool.wait_ge(wide_in[layer], (n + 1) * 16 * loads)
                        pool.nop(nofuse=True)
                        for u in range(G):
                            pool.indirect_dma_start(
                                z[:, 0, u, :], None, table,
                                bass.IndirectOffsetOnAxis(ap=idx[:, 0, u:u + 1], axis=0)).then_inc(wide_z[layer], 16)
            wide_gathers(0, h0_dram, 2)
            pool.wait_ge(folded0, GR)
            pool.memset(acc[0:D, 0, :], 0.0).then_inc(cleared, 1)
            pool.wait_ge(h_out, 32)
            pool.nop(nofuse=True)
            supertiles(pool, gathers(h1_dram, idx1_in, z1_in, msg1_ready))
            wide_gathers(1, h1_dram, 3)

        def node_columns(rows, blk, n):
            return acc[0:rows, blk, 0:N].rearrange("r (p j) -> r j p", p=NP)[:, bass.ds(n * JG, JG), :]

        @block.scalar
        def _(act):
            act.wait_ge(var_ready, 1)
            nc.scalar.activation(st_std[:], st_eps[:], ACT.Sqrt).then_inc(std_ready, 1)
            act.wait_ge(const_in, 16 * 7)
            nc.scalar.activation(si_sb[:], si_raw[:], ACT.Copy, scale=MUL ** -0.5).then_inc(si_scaled, 1)

            act.wait_ge(acc0_done, S)
            with if_wide(act):
                act.wait_ge(wide_free[0], S + 1)

            def stage0(n, k, first):
                if not first:
                    act.wait_ge(folded0, n - GU + 1)
                    act.nop(nofuse=True)
                nc.scalar.activation(stage[0:D, k, 0], node_columns(D, 0, n), ACT.Copy).then_inc(staged0, 1)
            groups(act, stage0)

            act.wait_ge(var_ready, 2)
            nc.scalar.activation(st_std[:], st_eps[:], ACT.Sqrt).then_inc(std_ready, 1)
            act.wait_ge(h_ready, 2)

            def stage_feat(n, k, first):
                if not first:
                    act.wait_ge(turned, n - GU + 1)
                    act.nop(nofuse=True)
                nc.scalar.activation(feat[:, k], big[0:NP, bass.ds(n * JG * D, JG * D)], ACT.Copy
                                     ).then_inc(feat_staged, 1)

            def copy_turned(n, k, first):
                act.wait_ge(turned, n + 1)
                if not first:
                    act.nop(nofuse=True)
                    act.wait_ge(si_done, n - GU + 1)
                nc.scalar.activation(stage[:, k, 0, 0, :], fold_ps[:, k, 0:NP], ACT.Copy
                                     ).then_inc(turned_copied, 1)

            def si_copies(n, k, first):
                stage_feat(n, k, first)
                copy_turned(n, k, first)
            groups(act, si_copies)

            def relu_halves(q):
                nc.scalar.activation(hid[0:HID, q, 0:HALF], hp_ps[0:HID, 0:HALF], ACT.Relu, bias=b1_sb[0:HID])
                nc.scalar.activation(hid[0:HID, q, HALF:SUP], hp_ps[HID:P, 0:HALF], ACT.Relu,
                                     bias=b1_sb[HID:P]).then_inc(hid_ready, 1)

            def relu(b, r, s):
                n = b * RING + r
                if s == 0:
                    act.wait_ge(ones_set, 1)
                act.wait_ge(hidpre_ready, n + 1)
                if s is None or s >= 2:
                    act.wait_ge(wts_ready, n - 1)
                relu_halves(r % 2)
            supertiles(act, relu)

            act.wait_ge(acc1_done, S)
            with if_wide(act):
                with act.Fori(0, S) as n:
                    act.wait_ge(hidpre_ready, n + S + 1)
                    act.nop(nofuse=True)
                    relu_halves(0)
                act.wait_ge(wide_free[1], S + 1)

            def stage1(n, k, first):
                if not first:
                    act.wait_ge(folded1, n - GU + 1)
                    act.nop(nofuse=True)
                for blk in range(2):
                    last = nc.scalar.activation(stage[:, k, blk], node_columns(P, blk, n), ACT.Copy)
                last.then_inc(staged1, 1)
            groups(act, stage1)

        @block.tensor
        def _(pe):
            def sum0(b, r, s):
                n = b * RING + r
                pe.wait_ge(msg0_ready, n + 1)
                if s is None or s >= 1:
                    pe.wait_ge(acc0_done, n)
                for u in range(G):
                    mm = pe.matmul(sums_ps[0:D, 0, :], z[:, r, u, :], onehot[:, r, u, :],
                                   start=(u == 0), stop=(u == G - 1))
                mm.then_inc(sum0_ready, 1)
            supertiles(pe, sum0)

            def wide_sums(layer, before, sums):
                with if_wide(pe):
                    with pe.Fori(0, S) as n:
                        before(n)
                        with pe.Fori(0, NWIN) as w:
                            pe.wait_ge(wide_hot[layer], n * NWIN + w + 1)
                            pe.nop(nofuse=True)
                            sums().then_inc(wide_sum[layer], 1)

            def wide_sums0():
                for u in range(G):
                    mm = pe.matmul(sums_ps[0:D, 0, :], z[:, 0, u, :], onehot[:, 0, u, :],
                                   start=(u == 0), stop=(u == G - 1))
                return mm
            wide_sums(0, lambda n: None, wide_sums0)

            pe.wait_ge(const_in, 16 * 7)

            def fold0(n, k, first):
                pe.wait_ge(staged0, n + 1)
                if not first:
                    pe.wait_ge(added0, n - GU + 1)
                for j in range(JG):
                    mm = pe.matmul(fold_ps[0:NP, k, j * D:(j + 1) * D], stage[0:D, k, 0, j, :], sel_sb[0:D, 0, :],
                                   start=True, stop=True)
                mm.then_inc(folded0, 1)
            groups(pe, fold0)

            pe.wait_ge(si_scaled, 1)
            pe.wait_ge(ones_set, 1)

            def self_interaction(n, k, first):
                pe.wait_ge(feat_staged, n + 1)
                if first:
                    pe.wait_ge(added0, GR)
                else:
                    pe.wait_ge(si_added, n - GU + 1)
                pe.transpose(fold_ps[:, k, 0:NP], feat[:, k], id_sb[0:NP, 0:NP]).then_inc(turned, 1)
                pe.wait_ge(turned_copied, n + 1)
                pe.matmul(fold_ps[0:NP, k, P:2 * P], stage[:, k, 0, 0, :], si_sb[:],
                          start=True, stop=True).then_inc(si_done, 1)
            groups(pe, self_interaction)

            def hidden(r):
                return pe.matmul(hp_ps[:, 0:HALF], w1_sb[:], ft_sb[:, r, :], start=True, stop=True)

            def weights(q):
                for u in range(G):
                    mm = pe.matmul(wts_ps[q][:, u, :], hid[:, q, u * P:(u + 1) * P], w2_sb[:],
                                   start=True, stop=True)
                return mm

            def window_sums(r):
                for u in range(G):
                    pe.matmul(sums_ps[:, 0, :], prod1[:, r % 2, u].rearrange("p i o -> p (i o)"),
                              onehot[:, r, u, :], start=(u == 0), stop=(u == G - 1))
                for u in range(G):
                    mm = pe.matmul(sums_ps[:, 1, :], prod2[:, r % 2, u, :], onehot[:, r, u, :],
                                   start=(u == 0), stop=(u == G - 1))
                return mm

            def edge_layer(b, r, s):
                n = b * RING + r
                if s is None or s >= 3:
                    v = (r - 3) % RING
                    pe.wait_ge(msg1_ready, n - 2)
                    if s is None or s >= 4:
                        pe.wait_ge(acc1_done, n - 3)
                    window_sums(v).then_inc(sum1_ready, 1)
                if s is None or 1 <= s <= S:
                    q = (r - 1) % 2
                    if s == 1:
                        pe.wait_ge(si_added, GR)
                    pe.wait_ge(hid_ready, n)
                    if s is None or s >= 3:
                        pe.wait_ge(wts_used, n - 2)
                    weights(q).then_inc(wts_ready, 1)
                if s is None or s < S:
                    pe.wait_ge(ft_in[r], (b + 1) * 16)
                    if s is None or s >= 1:
                        pe.wait_ge(hid_ready, n)
                    hidden(r).then_inc(hidpre_ready, 1)
            supertiles(pe, edge_layer, lag=3)

            def wide_weights(n):
                pe.wait_ge(wide_in[1], (n + 1) * 48)
                pe.nop(nofuse=True)
                hidden(0).then_inc(hidpre_ready, 1)
                pe.wait_ge(hid_ready, n + S + 1)
                pe.nop(nofuse=True)
                weights(0).then_inc(wts_ready, 1)
            wide_sums(1, wide_weights, lambda: window_sums(0))

            def fold1(n, k, first):
                pe.wait_ge(staged1, n + 1)
                if not first:
                    pe.wait_ge(added1, n - GU + 1)
                for j in range(JG):
                    for blk in range(2):
                        mm = pe.matmul(fold_ps[0:NP, k, j * D:(j + 1) * D], stage[:, k, blk, j, :],
                                       sel_sb[:, 1 + blk, :], start=(blk == 0), stop=(blk == 1))
                mm.then_inc(folded1, 1)
            groups(pe, fold1)

        @block.vector
        def _(dve):
            dve.wait_ge(dst_in, 16)
            dst_s = big[0:SPP, 0:SK * SUP].bitcast(I32).rearrange("p (k e) -> p k e", k=SK)
            nc.vector.tensor_reduce(least[:], dst_s, AX, ALU.min).then_inc(reduced, 1)
            nc.vector.tensor_reduce(most[:], dst_s, AX, ALU.max).then_inc(reduced, 1)
            dve.wait_ge(reduced, 2)
            nc.vector.tensor_copy(least_i[:], least[:]).then_inc(table_ready, 1)
            nc.vector.tensor_tensor(span_i[:], most[:], least[:], ALU.subtract).then_inc(table_ready, 1)

            nodes = [NP, J, D]

            def view(t):
                return t[0:NP, 0:J * D].rearrange("p (j d) -> p j d", d=D)

            def norm(turn):
                step = 4 * turn
                nc.vector.tensor_reduce(st_sum[:], view(x_sb), AX, ALU.add).then_inc(norm_step, 1)
                dve.wait_ge(norm_step, step + 1)
                nc.vector.tensor_scalar(st_neg[:], st_sum[:], -1.0 / D, None, ALU.mult).then_inc(norm_step, 1)
                dve.wait_ge(norm_step, step + 2)
                nc.vector.tensor_tensor(view(big), view(x_sb), st_neg[:].unsqueeze(2).to_broadcast(nodes),
                                        ALU.add).then_inc(norm_step, 1)
                dve.wait_ge(norm_step, step + 3)
                nc.vector.tensor_tensor(view(stage_flat), view(big), view(big), ALU.mult).then_inc(norm_step, 1)
                dve.wait_ge(norm_step, step + 4)
                nc.vector.tensor_reduce(st_var[:], view(stage_flat), AX, ALU.add).then_inc(reduced, 1)
                dve.wait_ge(reduced, 3 + turn * 2)
                nc.vector.tensor_scalar(st_eps[:], st_var[:], 1.0 / D, EPS, ALU.mult, ALU.add).then_inc(var_ready, 1)
                dve.wait_ge(std_ready, 1 + turn)
                nc.vector.reciprocal(st_inv[:], st_std[:]).then_inc(reduced, 1)
                dve.wait_ge(reduced, 4 + turn * 2)
                nc.vector.scalar_tensor_tensor(view(big), view(big), 0.0,
                                               st_inv[:].unsqueeze(2).to_broadcast(nodes),
                                               ALU.max, ALU.mult).then_inc(h_ready, 1)

            dve.wait_ge(x_in, 16)
            norm(0)

            dve.wait_ge(dstt_in, 16)
            dve.wait_ge(tab_in, 48)
            nc.vector.tensor_tensor(rel_sb[:].rearrange("p (s g) -> p s g", g=G),
                                    rel_sb[:].bitcast(I32).rearrange("p (s g) -> p s g", g=G),
                                    base_bc[:].unsqueeze(2).to_broadcast([P, S, G]),
                                    ALU.subtract).then_inc(rel_ready, 1)
            nc.vector.tensor_reduce(span_max[:], span_row[:], AX, ALU.max).then_inc(span_ready, 1)
            dve.wait_ge(rel_ready, 1)
            dve.wait_ge(const_in, 16 * 7)

            def tile_columns(t, n):
                return t[:, bass.ds(n * G, G)]

            def one_hots(n, r):
                return nc.vector.tensor_tensor(
                    onehot[:, r], iota_sb[:].unsqueeze(1).to_broadcast([P, G, WIN]),
                    tile_columns(rel_sb, n).unsqueeze(2).to_broadcast([P, G, WIN]), ALU.is_equal)

            def take_sums(n, s, ready, done, rows, blks):
                base = dve.value_load(base_row[0:1, bass.ds(n, 1)], min_val=0, max_val=N - 1)
                dve.wait_ge(ready, n + 1)
                if s is None or s >= 1:
                    dve.wait_ge(done, n)
                at = acc[0:rows, 0:blks, bass.ds(base, WIN)]
                nc.vector.tensor_tensor(at, at, sums_ps[0:rows, 0:blks, :], ALU.add).then_inc(done, 1)

            def layer0(b, r, s):
                n = b * RING + r
                if s is None or s < S:
                    if s is None or s >= RING:
                        dve.wait_ge(sum0_ready, n - RING + 1)
                    one_hots(n, r)
                    dve.wait_ge(z0_in[r], (b + 1) * 16 * G)
                    dve.wait_ge(ew_in[r], (b + 1) * 16)
                    nc.vector.tensor_tensor(z[:, r], z[:, r],
                                            ew_sb[:, r].unsqueeze(2).to_broadcast([P, G, D]),
                                            ALU.mult).then_inc(msg0_ready, 1)
                if s is None or s >= 1:
                    if s == 1:
                        dve.wait_ge(cleared, 2)
                    take_sums(n - 1, None if s is None else s - 1, sum0_ready, acc0_done, D, 1)
            supertiles(dve, layer0, lag=1)

            def wide_supertiles(layer, before, rows, blks, last_add):
                free, stepped, hot, summed = wide_free[layer], wide_step[layer], wide_hot[layer], wide_sum[layer]
                added = wide_added[layer]
                with if_wide(dve):
                    dve.wait_ge(last_add, S)
                    dve.nop(nofuse=True)
                    dve.engine_nop().then_inc(free, 1)
                    with dve.Fori(0, S) as n:
                        dve.wait_ge(wide_z[layer], (n + 1) * 16 * G)
                        dve.nop(nofuse=True)
                        before(n)
                        rel = tile_columns(rel_sb, n)
                        nc.vector.tensor_scalar(wide_near[:], rel, float(WIN), float(2 * AW), ALU.is_lt, ALU.mult
                                                ).then_inc(stepped, 1)
                        nc.vector.tensor_tensor(wide_dst[:], rel, base_bc[:, bass.ds(n, 1)].to_broadcast([P, G]),
                                                ALU.add).then_inc(stepped, 1)
                        dve.wait_ge(stepped, n * 3 + 2)
                        nc.vector.tensor_tensor(wide_dst[:], wide_dst[:], wide_near[:], ALU.add).then_inc(stepped, 1)
                        dve.wait_ge(stepped, n * 3 + 3)
                        dve.nop(nofuse=True)
                        with dve.Fori(0, NWIN) as w:
                            turn = n * NWIN + w
                            nc.vector.tensor_tensor(
                                onehot[:, 0], iota_sb[:].unsqueeze(1).to_broadcast([P, G, WIN]),
                                wide_dst[:].unsqueeze(2).to_broadcast([P, G, WIN]), ALU.is_equal).then_inc(hot, 1)
                            dve.wait_ge(summed, turn + 1)
                            dve.nop(nofuse=True)
                            nc.vector.tensor_scalar(wide_dst[:], wide_dst[:], float(-WIN), None, ALU.add
                                                    ).then_inc(added, 1)
                            at = acc[0:rows, 0:blks, bass.ds(w * WIN, WIN)]
                            nc.vector.tensor_tensor(at, at, sums_ps[0:rows, 0:blks, :], ALU.add).then_inc(added, 1)
                            dve.wait_ge(added, turn * 2 + 2)
                            dve.nop(nofuse=True)
                        dve.engine_nop().then_inc(free, 1)

            def wide_messages0(n):
                dve.wait_ge(wide_in[0], (n + 1) * 32)
                nc.vector.tensor_tensor(z[:, 0], z[:, 0], ew_sb[:, 0].unsqueeze(2).to_broadcast([P, G, D]),
                                        ALU.mult)
            wide_supertiles(0, wide_messages0, D, 1, acc0_done)

            def group_columns(n):
                return x_sb[:, bass.ds(n * JG * D, JG * D)]

            def add0(n, k, first):
                dve.wait_ge(folded0, n + 1)
                nc.vector.tensor_tensor(group_columns(n), group_columns(n), fold_ps[0:NP, k, 0:JG * D],
                                        ALU.add).then_inc(added0, 1)
            groups(dve, add0)
            dve.wait_ge(added0, GR)
            dve.wait_ge(h_out, 16)
            norm(1)

            def add_si(n, k, first):
                dve.wait_ge(si_done, n + 1)
                nc.vector.tensor_tensor(group_columns(n), group_columns(n), fold_ps[0:NP, k, P:P + JG * D],
                                        ALU.add).then_inc(si_added, 1)
            groups(dve, add_si)

            STEPS = 6

            def products(n, r, q, meanwhile):
                def step(i):
                    dve.wait_ge(prod_step, n * STEPS + i)

                wts = wts_ps[q]
                s_in, v_in = z[:, r, :, 0:MUL], z[:, r, :, MUL:D]
                sh0, sh1 = sh_sb[:, r, :, 0:1], sh_sb[:, r, :, 1:4]
                nc.vector.tensor_tensor(vsh[:], v_in.rearrange("p g (i m) -> p g i m", m=3),
                                        sh1.unsqueeze(2).to_broadcast([P, G, MUL, 3]), ALU.mult).then_inc(prod_step, 1)
                nc.vector.tensor_tensor(coef[:, :, MUL:], z[:, r], sh0.to_broadcast([P, G, D]),
                                        ALU.mult).then_inc(prod_step, 1)
                meanwhile()
                step(1)
                nc.vector.tensor_reduce(coef[:, :, 0:MUL], vsh[:], AX, ALU.add).then_inc(prod_step, 1)
                dve.wait_ge(wts_ready, n + 1)
                nc.vector.tensor_tensor(p011[:], wts[:, :, 2 * BLK:3 * BLK].rearrange("p g (i o) -> p g i o", i=MUL),
                                        s_in.unsqueeze(3).to_broadcast([P, G, MUL, MUL]), ALU.mult).then_inc(prod_step, 1)
                step(2)
                coef_v = coef[:, :, 2 * MUL:].rearrange("p g (i m) -> p g i m", m=3)
                for m in range(3):
                    last = nc.vector.tensor_tensor(
                        p101[:, :, :, m * MUL:(m + 1) * MUL],
                        wts[:, :, 3 * BLK:].rearrange("p g (i o) -> p g i o", i=MUL),
                        coef_v[:, :, :, m:m + 1].to_broadcast([P, G, MUL, MUL]), ALU.mult)
                last.then_inc(prod_step, 1)
                step(3)
                nc.vector.tensor_tensor(
                    prod1[:, q], wts[:, :, 0:2 * BLK].rearrange("p g (i o) -> p g i o", o=MUL),
                    coef[:, :, 0:2 * MUL].unsqueeze(3).to_broadcast([P, G, 2 * MUL, MUL]),
                    ALU.mult).then_inc(wts_used, 1)
                step(4)
                nc.vector.tensor_reduce(t011[:], p011[:].rearrange("p g i o -> p g o i"), AX, ALU.add
                                        ).then_inc(prod_step, 1)
                step(5)
                nc.vector.tensor_tensor(prod2[:, q, :, 0:HV].rearrange("p g (i c) -> p g i c", i=MUL // 2),
                                        p101[:, :, 0:MUL // 2], p101[:, :, MUL // 2:], ALU.add)
                step(6)
                nc.vector.tensor_tensor(prod2[:, q, :, HV:HV + 3 * MUL].rearrange("p g (m o) -> p g m o", m=3),
                                        t011[:].unsqueeze(2).to_broadcast([P, G, 3, MUL]),
                                        sh1.unsqueeze(3).to_broadcast([P, G, 3, MUL]), ALU.mult).then_inc(msg1_ready, 1)

            def layer1(b, r, s):
                n = b * RING + r
                if s == 0:
                    dve.wait_ge(pads_set, 1)
                if s is None or s < S:
                    if s is None or s >= 2:
                        dve.wait_ge(sum1_ready, n - 1)
                    dve.wait_ge(z1_in[r], (b + 1) * 16 * G)
                    dve.wait_ge(sh_in[r], (b + 1) * 16)
                    products(n, r, r % 2, lambda: one_hots(n, r))
                if s is None or s >= 1:
                    if s == 1:
                        dve.wait_ge(cleared, 5)
                    take_sums(n - 1, None if s is None else s - 1, sum1_ready, acc1_done, P, 2)
            supertiles(dve, layer1, lag=1)

            def wide_messages1(n):
                dve.wait_ge(wide_in[1], (n + 1) * 48)
                products(n + S, 0, 0, lambda: None)
            wide_supertiles(1, wide_messages1, P, 2, acc1_done)

            def add1(n, k, first):
                dve.wait_ge(folded1, n + 1)
                nc.vector.tensor_tensor(group_columns(n), group_columns(n), fold_ps[0:NP, k, 0:JG * D],
                                        ALU.add).then_inc(added1, 1)
            groups(dve, add1)


def kernel(**inputs):
    import numpy as np
    import concourse.bacc as bacc
    from concourse.bass_utils import run_bass_kernel_spmd

    a = {k: np.ascontiguousarray(v) for k, v in inputs.items()}
    N, E = a["x"].shape[0], a["src"].shape[0]
    S = E // SUP
    assert S * SUP == E

    w1 = a["L1_gnn_W1"]
    w1_2 = np.zeros((P, P), w1.dtype)
    w1_2[:D, :HID], w1_2[D:2 * D, HID:] = w1, w1
    b1_2 = np.concatenate([a["L1_gnn_b1"], a["L1_gnn_b1"]])[:, None]
    w2 = np.concatenate([a["L1_gnn_W2"], a["L1_gnn_b2"][None]]).reshape(HID + 1, 4, BLK)
    w2_aug = np.zeros((P, WN), w2.dtype)
    w2_aug[:HID + 1] = w2[:, [3, 0, 1, 2]].reshape(HID + 1, WN)
    si_mat = np.zeros((JG, D, JG, D), w1.dtype)
    for j in range(JG):
        si_mat[j, :MUL, j, :MUL] = a["L1_gnn_si_w0"]
        for m in range(3):
            si_mat[j, MUL + m::3, j, MUL + m::3] = a["L1_gnn_si_w1"]

    alpha, c110 = 0.25, 3 ** -0.5
    sel = np.zeros((P, 3, D), np.float32)
    sel[:D, 0] = np.eye(D)
    for i in range(2 * MUL):
        for o in range(MUL):
            sel[i * MUL + o, 1, o] = alpha * (c110 if i < MUL else 1.0)
    for c in range(HV + 3 * MUL):
        m, o = divmod(c % (3 * MUL), MUL)
        sel[c, 2, MUL + 3 * o + m] = alpha

    arrays = {
        "x": a["x"],
        "src_t": a["src"].reshape(S, G, P).transpose(0, 2, 1),
        "dst_flat": a["dst"],
        "dst_t": a["dst"].reshape(S * G, P).T,
        "ew_t": a["edge_weight"].reshape(S, G, P).transpose(0, 2, 1),
        "sh_t": a["edge_attr_4"].reshape(S, G, P, 4).transpose(0, 2, 1, 3).reshape(S, P, G * 4),
        "ft": a["edge_attr_32"].reshape(S, 2, HALF, D).transpose(0, 1, 3, 2).reshape(S, 2 * D, HALF),
        "w1_2": w1_2, "b1_2": b1_2, "w2_aug": w2_aug, "si_mat": si_mat.reshape(JG * D, JG * D),
        "iota": np.tile(np.arange(WIN, dtype=np.float32), (P, 1)),
        "ident": np.eye(P, dtype=np.float32),
        "sel": sel,
    }
    nc = bacc.Bacc("TRN2", target_bir_lowering=False, num_devices=1)
    sent, args = {}, []
    for name, v in arrays.items():
        v = np.ascontiguousarray(v)
        sent[f"in_{name}"] = v
        args.append(nc.dram_tensor(f"in_{name}", v.shape, mybir.dt.from_np(v.dtype), kind="ExternalInput").ap())
    args.append(nc.dram_tensor("out_0", (N, D), F32, kind="ExternalOutput").ap())
    gnn_two_layers(nc, *args)
    r = run_bass_kernel_spmd(nc, [sent], core_ids=[0])
    return r.results[0]["out_0"]
```

```python
from contextlib import ExitStack

import concourse.bass as bass
from concourse import mybir

P = 128
G = 5
SUP = G * P
HALF = SUP // 2
WIN = 64
RING = 4
MUL = 8
D = 4 * MUL
HID = 64
BLK = MUL * MUL
WN = 4 * BLK
HV = (MUL // 2) * 3 * MUL
PEG = 3
GB = 8
JG = 4
EPS = 1e-5

F32 = mybir.dt.float32
BF16 = mybir.dt.bfloat16
I32 = mybir.dt.int32
ALU = mybir.AluOpType
ACT = mybir.ActivationFunctionType
AX = mybir.AxisListType.X


def largest_divisor(n, most):
    return max(k for k in range(1, most + 1) if n % k == 0)


def gnn_two_layers(nc, x, src_t, src_flat, dst_flat, dst_t, ew_t, sh_t, ft, w1_2, b1_2, w2_aug, si_mat, iota,
                   lane, blocks, ident, sel, out):
    N = x.shape[0]
    S = src_t.shape[0]
    T = S * G
    NP = largest_divisor(N, 125)
    J = N // NP
    GR = J // JG
    GU = largest_divisor(GR, 5)
    SPP = largest_divisor(S, 125)
    SK = S // SPP
    FULL = S // RING
    NWIN = -(-N // WIN)
    AW = NWIN * WIN + WIN
    NC = -(-N // (GB * P))
    KD = NC * GB * D
    assert NC * D <= 512
    assert J % JG == 0 and FULL >= 2

    def uses(r):
        return FULL + (1 if r < S % RING else 0)

    def pool_tiles(r):
        return G - 1 if r < PEG else G

    def before(b, r, k):
        return b + (r - k) // RING, (r - k) % RING

    with ExitStack() as ctx:
        def sb(name, shape, dt=F32):
            return ctx.enter_context(nc.sbuf_tensor(name, shape, dt))

        def psum(name, shape):
            return ctx.enter_context(nc.psum_tensor(name, shape, F32))

        def sem(name):
            return ctx.enter_context(nc.semaphore(name))

        def sems(name):
            return [sem(f"{name}{r}") for r in range(RING)]

        h0_dram = nc.dram_tensor("h0_table", [N, D], F32).ap()
        h1_dram = nc.dram_tensor("h1_table", [N, D], F32).ap()
        base_dram = nc.dram_tensor("base_table", [S], I32).ap()
        span_dram = nc.dram_tensor("span_table", [S], I32).ap()

        w_ps = psum("w_ps", [P, 2, 3, 512])
        hp_ps = psum("hp_ps", [P, 512])
        sc_ps = psum("sc_ps", [P, 512])
        wts_ps = [w_ps[:, q].rearrange("p k n -> p (k n)")[:, 0:G * WN].rearrange("p (g n) -> p g n", g=G)
                  for q in range(2)]
        sums_ps = sc_ps[:, 0:2 * WIN].rearrange("p (k n) -> p k n", k=2)
        fold_ps = w_ps[:].rearrange("p q k n -> p (q k) n")

        acc = sb("acc", [P, 2, AW])
        x_sb = sb("x_sb", [NP, J * D])
        big = sb("big", [P, max(J * D, SK * SUP, KD)])
        st_sum, st_neg, st_var = (sb(n, [NP, J]) for n in ("st_sum", "st_neg", "st_var"))
        st_eps, st_std, st_inv = (sb(n, [NP, J]) for n in ("st_eps", "st_std", "st_inv"))
        stage_flat = sb("stage", [P, max(GU * 2 * JG * NP, J * D, 3 * KD // 2)])
        stage = stage_flat[:, 0:GU * 2 * JG * NP].rearrange("p (k b j n) -> p k b j n", k=GU, b=2, j=JG)
        feat = sb("feat", [P, max(GU, PEG), JG * D])
        rel_sb = sb("rel_sb", [P, T])
        base_row, span_row = sb("base_row", [1, S], I32), sb("span_row", [1, S], I32)
        span_max = sb("span_max", [1, 1], I32)
        base_bc = sb("base_bc", [P, S], I32)
        least, most = sb("least", [SPP, SK]), sb("most", [SPP, SK])
        least_i, span_i = sb("least_i", [SPP, SK], I32), sb("span_i", [SPP, SK], I32)
        iota_sb = sb("iota_sb", [P, WIN])
        lane_sb, block_sb = sb("lane_sb", [P, 1]), sb("block_sb", [P, GB])
        wide_dst, wide_near = sb("wide_dst", [P, G]), sb("wide_near", [P, G])
        id_sb = sb("id_sb", [P, P])
        sel_sb = sb("sel_sb", [P, 3, D])
        w1_sb = sb("w1_sb", [P, P])
        b1_sb = sb("b1_sb", [P, 1])
        w2_sb = sb("w2_sb", [P, WN])
        si_raw, si_sb = sb("si_raw", [JG * D, JG * D]), sb("si_sb", [JG * D, JG * D])
        idx = sb("idx", [P, RING, G], I32)
        ew_sb = sb("ew_sb", [P, RING, G])
        z = sb("z", [P, RING, G, D])
        onehot = sb("onehot", [P, RING, G, WIN])
        ft_sb = sb("ft_sb", [P, RING, HALF])
        sh_sb = sb("sh_sb", [P, RING, G, 4])
        hid = sb("hid", [P, 2, SUP])
        coef = sb("coef", [P, G, MUL + D])
        vsh = sb("vsh", [P, G, MUL, 3])
        p011 = sb("p011", [P, G, MUL, MUL])
        t011 = sb("t011", [P, G, MUL])
        p101 = sb("p101", [P, G, MUL, 3 * MUL])
        prod1 = sb("prod1", [P, 2, G, 2 * MUL, MUL])
        prod2 = sb("prod2", [P, 2, G, P])

        parts = stage_flat[:, 0:3 * KD // 2].bitcast(BF16).rearrange("p (t c b d) -> p t c b d", t=3, c=NC, b=GB)
        table = big[:, 0:KD]
        pick = [t[:, 0:GB * P // 2].bitcast(BF16).rearrange("p (b e) -> p b e", b=GB) for t in (
            prod1[:, 0].rearrange("p g i o -> p (g i o)"), prod1[:, 1].rearrange("p g i o -> p (g i o)"),
            prod2[:, 0].rearrange("p g c -> p (g c)"))]
        group_prod = p101[:].rearrange("p g i c -> p (g i c)")[:, 0:NC * D].rearrange("p (c d) -> p c d", d=D)
        key_in, key = feat[:].bitcast(I32), feat
        group_id, group_hot = sb("group_id", [P, 1], I32), sb("group_hot", [P, NC])

        x_in, dst_in, dstt_in, const_in = (
            sem(n) for n in ("x_in", "dst_in", "dstt_in", "const_in"))
        reduced, table_ready, tab_out, tab_in, rel_ready = (
            sem(n) for n in ("reduced", "table_ready", "tab_out", "tab_in", "rel_ready"))
        cleared, ones_set, pads_set = sem("cleared"), sem("ones_set"), sem("pads_set")
        norm_step, var_ready, std_ready, h_ready, h_out = (
            sem(n) for n in ("norm_step", "var_ready", "std_ready", "h_ready", "h_out"))
        staged0, folded0, added0 = sem("staged0"), sem("folded0"), sem("added0")
        staged1, folded1, added1, res_out = sem("staged1"), sem("folded1"), sem("added1"), sem("res_out")
        si_scaled, feat_staged, turned, turned_copied, si_done, si_added = (
            sem(n) for n in ("si_scaled", "feat_staged", "turned", "turned_copied", "si_done", "si_added"))
        idx0_in, z0_in, ew_in = sems("idx0_in"), sems("z0_in"), sems("ew_in")
        msg0_ready, sum0_ready, acc0_done = sem("msg0_ready"), sem("sum0_ready"), sem("acc0_done")
        keys_in = [sem(f"keys_in{r}") for r in range(PEG)]
        table_padded, table_in, split_act, split_dve = (
            sem(n) for n in ("table_padded", "table_in", "split_act", "split_dve"))
        key_step, pick_ready, picked, group_step = (
            sem(n) for n in ("key_step", "pick_ready", "picked", "group_step"))
        idx1_in, z1_in, sh_in, ft_in = sems("idx1_in"), sems("z1_in"), sems("sh_in"), sems("ft_in")
        hidpre_ready, hid_ready, wts_ready, wts_used = (
            sem(n) for n in ("hidpre_ready", "hid_ready", "wts_ready", "wts_used"))
        prod_step, msg1_ready, sum1_ready, acc1_done = (
            sem(n) for n in ("prod_step", "msg1_ready", "sum1_ready", "acc1_done"))

        def supertiles(eng, body, lag=0):
            for s in range(RING):
                body(0, s, s)
            with eng.Fori(1, FULL) as b:
                for r in range(RING):
                    body(b, r, None)
            for s in range(FULL * RING, S + lag):
                body(s // RING, s % RING, s)

        def groups(eng, body):
            for k in range(GU):
                body(k, k, True)
            if GR > GU:
                with eng.Fori(1, GR // GU) as g:
                    for k in range(GU):
                        body(g * GU + k, k, False)

        span_ready = sem("span_ready")
        wide_free, wide_in, wide_z = ([sem(f"{n}{layer}") for layer in (0, 1)] for n in ("wide_free", "wide_in", "wide_z"))
        wide_step, wide_hot, wide_sum = ([sem(f"{n}{layer}") for layer in (0, 1)] for n in ("wide_step", "wide_hot", "wide_sum"))
        wide_added = [sem("wide_added0"), sem("wide_added1")]

        def if_wide(eng):
            eng.wait_ge(span_ready, 1)
            return eng.If(eng.value_load(span_max[0:1, 0:1], min_val=0, max_val=N - 1) >= WIN)

        block = ctx.enter_context(nc.Block())

        @block.sync
        def _(sp):
            sp.dma_start(big[0:SPP, 0:SK * SUP].bitcast(I32),
                         dst_flat.rearrange("(p e) -> p e", p=SPP)).then_inc(dst_in, 16)
            sp.dma_start(x_sb[:], x.rearrange("(p j) d -> p (j d)", p=NP)).then_inc(x_in, 16)
            sp.dma_start(rel_sb[:].bitcast(I32), dst_t).then_inc(dstt_in, 16)
            for to, of in ((iota_sb, iota), (lane_sb, lane), (block_sb, blocks), (id_sb, ident), (sel_sb, sel), (w1_sb, w1_2), (b1_sb, b1_2),
                           (w2_sb, w2_aug), (si_raw, si_mat)):
                sp.dma_start(to[:], of).then_inc(const_in, 16)
            sp.wait_ge(table_ready, 2)
            sp.dma_start(base_dram.rearrange("(p k) -> p k", p=SPP), least_i[:]).then_inc(tab_out, 16)
            sp.dma_start(span_dram.rearrange("(p k) -> p k", p=SPP), span_i[:]).then_inc(tab_out, 16)
            sp.wait_ge(tab_out, 32)
            sp.dma_start(base_row[:], base_dram.rearrange("(a s) -> a s", a=1)).then_inc(tab_in, 16)
            sp.dma_start(span_row[:], span_dram.rearrange("(a s) -> a s", a=1)).then_inc(tab_in, 16)
            sp.dma_start(base_bc[:], base_dram.rearrange("(a s) -> a s", a=1).to_broadcast([P, S])
                         ).then_inc(tab_in, 16)
            sp.wait_ge(h_ready, 1)
            sp.dma_start(h0_dram.rearrange("(p j) d -> p (j d)", p=NP), big[0:NP, 0:J * D]).then_inc(h_out, 16)

            whole = N // P * P
            sp.wait_ge(h_out, 16)
            sp.wait_ge(table_padded, 1)
            sp.dma_start(table[:, 0:whole // P * D].rearrange("a (k d) -> a k d", d=D),
                         h0_dram[0:whole].rearrange("(k a) d -> a k d", a=P)).then_inc(table_in, 16)
            if whole < N:
                sp.dma_start(table[0:N - whole, whole // P * D:(whole // P + 1) * D], h0_dram[whole:N]
                             ).then_inc(table_in, 16)

            def load0(b, r, s):
                n = b * RING + r
                if s is None or s >= RING:
                    sp.wait_ge(z0_in[r], b * 16 * pool_tiles(r))
                    sp.nop(nofuse=True)
                    sp.wait_ge(msg0_ready, n - RING + 1)
                    sp.nop(nofuse=True)
                sp.dma_start(idx[:, r, :], src_t[n]).then_inc(idx0_in[r], 16)
                sp.dma_start(ew_sb[:, r, :], ew_t[n]).then_inc(ew_in[r], 16)
                if r < PEG:
                    sp.dma_start(key_in[:, r, :], src_flat[n, :, (G - 1) * P:G * P].to_broadcast([P, P])
                                 ).then_inc(keys_in[r], 16)
            supertiles(sp, load0)

            def wide_loads(layer, loads):
                with if_wide(sp):
                    with sp.Fori(0, S) as n:
                        sp.wait_ge(wide_free[layer], n + 1)
                        for to, of in loads:
                            sp.dma_start(to, of[n]).then_inc(wide_in[layer], 16)
                    sp.wait_ge(wide_free[layer], S + 1)
            wide_loads(0, [(idx[:, 0, :], src_t), (ew_sb[:, 0, :], ew_t)])

            sp.wait_ge(h_ready, 2)
            sp.dma_start(h1_dram.rearrange("(p j) d -> p (j d)", p=NP), big[0:NP, 0:J * D]).then_inc(h_out, 16)

            def load1(b, r, s):
                n = b * RING + r
                if s is not None and s < RING:
                    sp.wait_ge(z0_in[r], uses(r) * 16 * pool_tiles(r))
                else:
                    sp.wait_ge(z1_in[r], b * 16 * G)
                sp.dma_start(idx[:, r, :], src_t[n]).then_inc(idx1_in[r], 16)
                if s is None or s >= RING:
                    sp.wait_ge(hidpre_ready, n - RING + 1)
                sp.dma_start(ft_sb[0:2 * D, r, :], ft[n]).then_inc(ft_in[r], 16)
                if s is None or s >= RING:
                    sp.wait_ge(msg1_ready, n - RING + 1)
                sp.dma_start(sh_sb[:, r].rearrange("p g c -> p (g c)"), sh_t[n]).then_inc(sh_in[r], 16)
            supertiles(sp, load1)
            wide_loads(1, [(idx[:, 0, :], src_t), (ft_sb[0:2 * D, 0, :], ft), (sh_sb[:, 0].rearrange("p g c -> p (g c)"), sh_t)])

            sp.wait_ge(added1, GR)
            sp.dma_start(out.rearrange("(p j) d -> p (j d)", p=NP), x_sb[:]).then_inc(res_out, 16)
            sp.wait_ge(res_out, 16)

        @block.gpsimd
        def _(pool):
            pool.memset(acc[:, 0, :], 0.0).then_inc(cleared, 1)
            pool.memset(acc[:, 1, :], 0.0).then_inc(cleared, 1)
            pool.wait_ge(cleared, 2)
            pool.memset(ft_sb[2 * D:], 0.0).then_inc(cleared, 1)
            pool.wait_ge(cleared, 3)
            pool.memset(hid[HID:], 0.0).then_inc(cleared, 1)
            pool.wait_ge(cleared, 4)
            pool.memset(hid[HID:HID + 1], 1.0).then_inc(ones_set, 1)

            def gathers(rows, idx_in, z_in, used, tiles):
                def gather(b, r, s):
                    n = b * RING + r
                    pool.wait_ge(idx_in[r], (b + 1) * 16)
                    if s is None or s >= RING:
                        pool.nop(nofuse=True)
                        pool.wait_ge(used, n - RING + 1)
                    pool.nop(nofuse=True)
                    for u in range(tiles(r)):
                        pool.indirect_dma_start(
                            z[:, r, u, :], None, rows,
                            bass.IndirectOffsetOnAxis(ap=idx[:, r, u:u + 1], axis=0)).then_inc(z_in[r], 16)
                return gather

            pool.wait_ge(ones_set, 1)
            pool.nop(nofuse=True)
            pool.wait_ge(h_out, 16)
            pool.nop(nofuse=True)
            supertiles(pool, gathers(h0_dram, idx0_in, z0_in, sum0_ready, pool_tiles))

            def wide_gathers(layer, rows, loads):
                with if_wide(pool):
                    with pool.Fori(0, S) as n:
                        pool.wait_ge(wide_in[layer], (n + 1) * 16 * loads)
                        pool.nop(nofuse=True)
                        for u in range(G):
                            pool.indirect_dma_start(
                                z[:, 0, u, :], None, rows,
                                bass.IndirectOffsetOnAxis(ap=idx[:, 0, u:u + 1], axis=0)).then_inc(wide_z[layer], 16)
            wide_gathers(0, h0_dram, 2)
            pool.wait_ge(folded0, GR)
            pool.memset(prod2[:, :, :, HV + 3 * MUL:P], 0.0).then_inc(pads_set, 1)
            pool.wait_ge(pads_set, 1)
            pool.memset(acc[0:D, 0, :], 0.0).then_inc(cleared, 1)
            pool.wait_ge(h_out, 32)
            pool.nop(nofuse=True)
            supertiles(pool, gathers(h1_dram, idx1_in, z1_in, msg1_ready, lambda r: G))
            wide_gathers(1, h1_dram, 3)

        def node_columns(rows, blk, n):
            return acc[0:rows, blk, 0:N].rearrange("r (p j) -> r j p", p=NP)[:, bass.ds(n * JG, JG), :]

        @block.scalar
        def _(act):
            act.wait_ge(var_ready, 1)
            nc.scalar.activation(st_std[:], st_eps[:], ACT.Sqrt).then_inc(std_ready, 1)
            act.wait_ge(const_in, 16 * 9)
            nc.scalar.activation(si_sb[:], si_raw[:], ACT.Copy, scale=MUL ** -0.5).then_inc(si_scaled, 1)

            act.wait_ge(table_in, 16 * (1 + (N % P > 0)))
            flat = parts.rearrange("p t c b d -> p t (c b d)")
            nc.scalar.activation(flat[:, 0], table, ACT.Copy).then_inc(split_act, 1)
            act.wait_ge(split_dve, 1)
            nc.scalar.activation(flat[:, 1], table, ACT.Copy).then_inc(split_act, 1)

            act.wait_ge(acc0_done, S)
            with if_wide(act):
                act.wait_ge(wide_free[0], S + 1)

            def stage0(n, k, first):
                if not first:
                    act.wait_ge(folded0, n - GU + 1)
                    act.nop(nofuse=True)
                nc.scalar.activation(stage[0:D, k, 0], node_columns(D, 0, n), ACT.Copy).then_inc(staged0, 1)
            groups(act, stage0)

            act.wait_ge(var_ready, 2)
            nc.scalar.activation(st_std[:], st_eps[:], ACT.Sqrt).then_inc(std_ready, 1)
            act.wait_ge(h_ready, 2)

            def stage_feat(n, k, first):
                if not first:
                    act.wait_ge(turned, n - GU + 1)
                    act.nop(nofuse=True)
                nc.scalar.activation(feat[0:NP, k], big[0:NP, bass.ds(n * JG * D, JG * D)], ACT.Copy
                                     ).then_inc(feat_staged, 1)

            def copy_turned(n, k, first):
                act.wait_ge(turned, n + 1)
                if not first:
                    act.nop(nofuse=True)
                    act.wait_ge(si_done, n - GU + 1)
                nc.scalar.activation(stage[:, k, 0, 0, :], fold_ps[:, k, 0:NP], ACT.Copy
                                     ).then_inc(turned_copied, 1)

            def si_copies(n, k, first):
                stage_feat(n, k, first)
                copy_turned(n, k, first)
            groups(act, si_copies)

            def relu_halves(q):
                nc.scalar.activation(hid[0:HID, q, 0:HALF], hp_ps[0:HID, 0:HALF], ACT.Relu, bias=b1_sb[0:HID])
                nc.scalar.activation(hid[0:HID, q, HALF:SUP], hp_ps[HID:P, 0:HALF], ACT.Relu,
                                     bias=b1_sb[HID:P]).then_inc(hid_ready, 1)

            def relu(b, r, s):
                n = b * RING + r
                if s == 0:
                    act.wait_ge(ones_set, 1)
                act.wait_ge(hidpre_ready, n + 1)
                if s is None or s >= 2:
                    act.wait_ge(wts_ready, n - 1)
                relu_halves(r % 2)
            supertiles(act, relu)

            act.wait_ge(acc1_done, S)
            with if_wide(act):
                with act.Fori(0, S) as n:
                    act.wait_ge(hidpre_ready, n + S + 1)
                    act.nop(nofuse=True)
                    relu_halves(0)
                act.wait_ge(wide_free[1], S + 1)

            def stage1(n, k, first):
                if not first:
                    act.wait_ge(folded1, n - GU + 1)
                    act.nop(nofuse=True)
                for blk in range(2):
                    last = nc.scalar.activation(stage[:, k, blk], node_columns(P, blk, n), ACT.Copy)
                last.then_inc(staged1, 1)
            groups(act, stage1)

        @block.tensor
        def _(pe):
            def sum0(b, r, s):
                n = b * RING + r
                if s == 0:
                    pe.wait_ge(split_dve, 2)
                if r < PEG and (s is None or s < S):
                    pe.wait_ge(pick_ready, b * PEG + r + 1)
                    for blk in range(GB):
                        for t in range(3):
                            mm = pe.matmul(fold_ps[:, r, 0:NC * D], pick[r][:, blk, :], parts[:, t, :, blk, :],
                                           start=(blk == 0 and t == 0), stop=(blk == GB - 1 and t == 2))
                    mm.then_inc(picked, 1)
                if s is None or s >= 2:
                    v = (r - 2) % RING
                    pe.wait_ge(msg0_ready, n - 1)
                    if s is None or s >= 3:
                        pe.wait_ge(acc0_done, n - 2)
                    for u in range(G):
                        mm = pe.matmul(sums_ps[0:D, 0, :], z[:, v, u, :], onehot[:, v, u, :],
                                       start=(u == 0), stop=(u == G - 1))
                    mm.then_inc(sum0_ready, 1)
            supertiles(pe, sum0, lag=2)

            def wide_sums(layer, before, sums):
                with if_wide(pe):
                    with pe.Fori(0, S) as n:
                        before(n)
                        with pe.Fori(0, NWIN) as w:
                            pe.wait_ge(wide_hot[layer], n * NWIN + w + 1)
                            pe.nop(nofuse=True)
                            sums().then_inc(wide_sum[layer], 1)

            def wide_sums0():
                for u in range(G):
                    mm = pe.matmul(sums_ps[0:D, 0, :], z[:, 0, u, :], onehot[:, 0, u, :],
                                   start=(u == 0), stop=(u == G - 1))
                return mm
            wide_sums(0, lambda n: None, wide_sums0)

            pe.wait_ge(const_in, 16 * 9)

            def fold0(n, k, first):
                pe.wait_ge(staged0, n + 1)
                if not first:
                    pe.wait_ge(added0, n - GU + 1)
                for j in range(JG):
                    mm = pe.matmul(fold_ps[0:NP, k, j * D:(j + 1) * D], stage[0:D, k, 0, j, :], sel_sb[0:D, 0, :],
                                   start=True, stop=True)
                mm.then_inc(folded0, 1)
            groups(pe, fold0)

            pe.wait_ge(si_scaled, 1)
            pe.wait_ge(ones_set, 1)

            def self_interaction(n, k, first):
                pe.wait_ge(feat_staged, n + 1)
                if first:
                    pe.wait_ge(added0, GR)
                else:
                    pe.wait_ge(si_added, n - GU + 1)
                pe.transpose(fold_ps[:, k, 0:NP], feat[0:NP, k], id_sb[0:NP, 0:NP]).then_inc(turned, 1)
                pe.wait_ge(turned_copied, n + 1)
                pe.matmul(fold_ps[0:NP, k, P:2 * P], stage[:, k, 0, 0, :], si_sb[:],
                          start=True, stop=True).then_inc(si_done, 1)
            groups(pe, self_interaction)

            def hidden(r):
                return pe.matmul(hp_ps[:, 0:HALF], w1_sb[:], ft_sb[:, r, :], start=True, stop=True)

            def weights(q):
                for u in range(G):
                    mm = pe.matmul(wts_ps[q][:, u, :], hid[:, q, u * P:(u + 1) * P], w2_sb[:],
                                   start=True, stop=True)
                return mm

            def window_sums(r):
                for u in range(G):
                    pe.matmul(sums_ps[:, 0, :], prod1[:, r % 2, u].rearrange("p i o -> p (i o)"),
                              onehot[:, r, u, :], start=(u == 0), stop=(u == G - 1))
                for u in range(G):
                    mm = pe.matmul(sums_ps[:, 1, :], prod2[:, r % 2, u, :], onehot[:, r, u, :],
                                   start=(u == 0), stop=(u == G - 1))
                return mm

            def edge_layer(b, r, s):
                n = b * RING + r
                if s is None or s >= 3:
                    v = (r - 3) % RING
                    pe.wait_ge(msg1_ready, n - 2)
                    if s is None or s >= 4:
                        pe.wait_ge(acc1_done, n - 3)
                    window_sums(v).then_inc(sum1_ready, 1)
                if s is None or 1 <= s <= S:
                    q = (r - 1) % 2
                    if s == 1:
                        pe.wait_ge(si_added, GR)
                    pe.wait_ge(hid_ready, n)
                    if s is None or s >= 3:
                        pe.wait_ge(wts_used, n - 2)
                    weights(q).then_inc(wts_ready, 1)
                if s is None or s < S:
                    pe.wait_ge(ft_in[r], (b + 1) * 16)
                    if s is None or s >= 1:
                        pe.wait_ge(hid_ready, n)
                    hidden(r).then_inc(hidpre_ready, 1)
            supertiles(pe, edge_layer, lag=3)

            def wide_weights(n):
                pe.wait_ge(wide_in[1], (n + 1) * 48)
                pe.nop(nofuse=True)
                hidden(0).then_inc(hidpre_ready, 1)
                pe.wait_ge(hid_ready, n + S + 1)
                pe.nop(nofuse=True)
                weights(0).then_inc(wts_ready, 1)
            wide_sums(1, wide_weights, lambda: window_sums(0))

            def fold1(n, k, first):
                pe.wait_ge(staged1, n + 1)
                if not first:
                    pe.wait_ge(added1, n - GU + 1)
                for j in range(JG):
                    for blk in range(2):
                        mm = pe.matmul(fold_ps[0:NP, k, j * D:(j + 1) * D], stage[:, k, blk, j, :],
                                       sel_sb[:, 1 + blk, :], start=(blk == 0), stop=(blk == 1))
                mm.then_inc(folded1, 1)
            groups(pe, fold1)

        @block.vector
        def _(dve):
            dve.wait_ge(dst_in, 16)
            dst_s = big[0:SPP, 0:SK * SUP].bitcast(I32).rearrange("p (k e) -> p k e", k=SK)
            nc.vector.tensor_reduce(least[:], dst_s, AX, ALU.min).then_inc(reduced, 1)
            nc.vector.tensor_reduce(most[:], dst_s, AX, ALU.max).then_inc(reduced, 1)
            dve.wait_ge(reduced, 2)
            nc.vector.tensor_copy(least_i[:], least[:]).then_inc(table_ready, 1)
            nc.vector.tensor_tensor(span_i[:], most[:], least[:], ALU.subtract).then_inc(table_ready, 1)

            nodes = [NP, J, D]

            def view(t):
                return t[0:NP, 0:J * D].rearrange("p (j d) -> p j d", d=D)

            def norm(turn):
                step = 4 * turn
                nc.vector.tensor_reduce(st_sum[:], view(x_sb), AX, ALU.add).then_inc(norm_step, 1)
                dve.wait_ge(norm_step, step + 1)
                nc.vector.tensor_scalar(st_neg[:], st_sum[:], -1.0 / D, None, ALU.mult).then_inc(norm_step, 1)
                dve.wait_ge(norm_step, step + 2)
                nc.vector.tensor_tensor(view(big), view(x_sb), st_neg[:].unsqueeze(2).to_broadcast(nodes),
                                        ALU.add).then_inc(norm_step, 1)
                dve.wait_ge(norm_step, step + 3)
                nc.vector.tensor_tensor(view(stage_flat), view(big), view(big), ALU.mult).then_inc(norm_step, 1)
                dve.wait_ge(norm_step, step + 4)
                nc.vector.tensor_reduce(st_var[:], view(stage_flat), AX, ALU.add).then_inc(reduced, 1)
                dve.wait_ge(reduced, 3 + turn * 2)
                nc.vector.tensor_scalar(st_eps[:], st_var[:], 1.0 / D, EPS, ALU.mult, ALU.add).then_inc(var_ready, 1)
                dve.wait_ge(std_ready, 1 + turn)
                nc.vector.reciprocal(st_inv[:], st_std[:]).then_inc(reduced, 1)
                dve.wait_ge(reduced, 4 + turn * 2)
                nc.vector.scalar_tensor_tensor(view(big), view(big), 0.0,
                                               st_inv[:].unsqueeze(2).to_broadcast(nodes),
                                               ALU.max, ALU.mult).then_inc(h_ready, 1)

            dve.wait_ge(x_in, 16)
            norm(0)

            dve.wait_ge(dstt_in, 16)
            dve.wait_ge(tab_in, 48)
            nc.vector.tensor_tensor(rel_sb[:].rearrange("p (s g) -> p s g", g=G),
                                    rel_sb[:].bitcast(I32).rearrange("p (s g) -> p s g", g=G),
                                    base_bc[:].unsqueeze(2).to_broadcast([P, S, G]),
                                    ALU.subtract).then_inc(rel_ready, 1)
            nc.vector.tensor_reduce(span_max[:], span_row[:], AX, ALU.max).then_inc(span_ready, 1)
            dve.wait_ge(rel_ready, 1)
            dve.wait_ge(const_in, 16 * 9)

            dve.wait_ge(h_out, 16)
            nc.vector.memset(table[:, N // P * D:KD], 0.0).then_inc(table_padded, 1)
            flat = parts.rearrange("p t c b d -> p t (c b d)")
            dve.wait_ge(split_act, 1)
            nc.vector.tensor_tensor(table, table, flat[:, 0], ALU.subtract).then_inc(split_dve, 1)
            dve.wait_ge(split_act, 2)
            nc.vector.tensor_tensor(flat[:, 2], table, flat[:, 1], ALU.subtract).then_inc(split_dve, 1)

            def tile_columns(t, n):
                return t[:, bass.ds(n * G, G)]

            def one_hots(n, r):
                return nc.vector.tensor_tensor(
                    onehot[:, r], iota_sb[:].unsqueeze(1).to_broadcast([P, G, WIN]),
                    tile_columns(rel_sb, n).unsqueeze(2).to_broadcast([P, G, WIN]), ALU.is_equal)

            def take_sums(n, s, ready, done, rows, blks):
                base = dve.value_load(base_row[0:1, bass.ds(n, 1)], min_val=0, max_val=N - 1)
                dve.wait_ge(ready, n + 1)
                if s is None or s >= 1:
                    dve.wait_ge(done, n)
                at = acc[0:rows, 0:blks, bass.ds(base, WIN)]
                nc.vector.tensor_tensor(at, at, sums_ps[0:rows, 0:blks, :], ALU.add).then_inc(done, 1)

            def make_pick(b, r, s):
                done = b * PEG + r
                dve.wait_ge(keys_in[r], (b + 1) * 16)
                nc.vector.tensor_scalar(key_in[:, r], key_in[:, r], GB * P - 1, None, ALU.bitwise_and
                                        ).then_inc(key_step, 1)
                dve.wait_ge(key_step, done * 2 + 1)
                nc.vector.tensor_scalar(key[:, r], key_in[:, r], lane_sb[:], None, ALU.subtract).then_inc(key_step, 1)
                dve.wait_ge(key_step, done * 2 + 2)
                if s is None or s >= RING:
                    dve.wait_ge(picked, b * PEG + r - PEG + 1)
                nc.vector.tensor_tensor(pick[r], key[:, r].unsqueeze(1).to_broadcast([P, GB, P]),
                                        block_sb[:].unsqueeze(2).to_broadcast([P, GB, P]), ALU.is_equal
                                        ).then_inc(pick_ready, 1)

            def select_group(b, r):
                done = (b * PEG + r) * 4
                dve.wait_ge(idx0_in[r], (b + 1) * 16)
                nc.vector.tensor_scalar(group_id[:], idx[:, r, G - 1:G], (GB * P).bit_length() - 1, None,
                                        ALU.logical_shift_right).then_inc(group_step, 1)
                dve.wait_ge(group_step, done + 1)
                nc.vector.tensor_tensor(group_hot[:], iota_sb[:, 0:NC], group_id[:].to_broadcast([P, NC]),
                                        ALU.is_equal).then_inc(group_step, 1)
                dve.wait_ge(group_step, done + 2)
                dve.wait_ge(picked, b * PEG + r + 1)
                nc.vector.tensor_tensor(group_prod, fold_ps[:, r, 0:NC * D].rearrange("p (c d) -> p c d", d=D),
                                        group_hot[:].unsqueeze(2).to_broadcast([P, NC, D]), ALU.mult
                                        ).then_inc(group_step, 1)
                dve.wait_ge(group_step, done + 3)
                nc.vector.tensor_reduce(z[:, r, G - 1, :], group_prod.rearrange("p c d -> p d c"), AX, ALU.add
                                        ).then_inc(group_step, 1)
                dve.wait_ge(group_step, done + 4)

            def layer0(b, r, s):
                n = b * RING + r
                if r < PEG and (s is None or s < S):
                    make_pick(b, r, s)
                if s is None or 2 <= s <= S + 1:
                    bv, v = before(b, r, 2)
                    one_hots(n - 2, v)
                    if v < PEG:
                        select_group(bv, v)
                    dve.wait_ge(z0_in[v], (bv + 1) * 16 * pool_tiles(v))
                    dve.wait_ge(ew_in[v], (bv + 1) * 16)
                    nc.vector.tensor_tensor(z[:, v], z[:, v], ew_sb[:, v].unsqueeze(2).to_broadcast([P, G, D]),
                                            ALU.mult).then_inc(msg0_ready, 1)
                if s is None or s >= 3:
                    if s == 3:
                        dve.wait_ge(cleared, 2)
                    take_sums(n - 3, None if s is None else s - 3, sum0_ready, acc0_done, D, 1)
            supertiles(dve, layer0, lag=3)

            def wide_supertiles(layer, before, rows, blks, last_add):
                free, stepped, hot, summed = wide_free[layer], wide_step[layer], wide_hot[layer], wide_sum[layer]
                added = wide_added[layer]
                with if_wide(dve):
                    dve.wait_ge(last_add, S)
                    dve.nop(nofuse=True)
                    dve.engine_nop().then_inc(free, 1)
                    with dve.Fori(0, S) as n:
                        dve.wait_ge(wide_z[layer], (n + 1) * 16 * G)
                        dve.nop(nofuse=True)
                        before(n)
                        rel = tile_columns(rel_sb, n)
                        nc.vector.tensor_scalar(wide_near[:], rel, float(WIN), float(2 * AW), ALU.is_lt, ALU.mult
                                                ).then_inc(stepped, 1)
                        nc.vector.tensor_tensor(wide_dst[:], rel, base_bc[:, bass.ds(n, 1)].to_broadcast([P, G]),
                                                ALU.add).then_inc(stepped, 1)
                        dve.wait_ge(stepped, n * 3 + 2)
                        nc.vector.tensor_tensor(wide_dst[:], wide_dst[:], wide_near[:], ALU.add).then_inc(stepped, 1)
                        dve.wait_ge(stepped, n * 3 + 3)
                        dve.nop(nofuse=True)
                        with dve.Fori(0, NWIN) as w:
                            turn = n * NWIN + w
                            nc.vector.tensor_tensor(
                                onehot[:, 0], iota_sb[:].unsqueeze(1).to_broadcast([P, G, WIN]),
                                wide_dst[:].unsqueeze(2).to_broadcast([P, G, WIN]), ALU.is_equal).then_inc(hot, 1)
                            dve.wait_ge(summed, turn + 1)
                            dve.nop(nofuse=True)
                            nc.vector.tensor_scalar(wide_dst[:], wide_dst[:], float(-WIN), None, ALU.add
                                                    ).then_inc(added, 1)
                            at = acc[0:rows, 0:blks, bass.ds(w * WIN, WIN)]
                            nc.vector.tensor_tensor(at, at, sums_ps[0:rows, 0:blks, :], ALU.add).then_inc(added, 1)
                            dve.wait_ge(added, turn * 2 + 2)
                            dve.nop(nofuse=True)
                        dve.engine_nop().then_inc(free, 1)

            def wide_messages0(n):
                dve.wait_ge(wide_in[0], (n + 1) * 32)
                nc.vector.tensor_tensor(z[:, 0], z[:, 0], ew_sb[:, 0].unsqueeze(2).to_broadcast([P, G, D]),
                                        ALU.mult)
            wide_supertiles(0, wide_messages0, D, 1, acc0_done)

            def group_columns(n):
                return x_sb[:, bass.ds(n * JG * D, JG * D)]

            def add0(n, k, first):
                dve.wait_ge(folded0, n + 1)
                nc.vector.tensor_tensor(group_columns(n), group_columns(n), fold_ps[0:NP, k, 0:JG * D],
                                        ALU.add).then_inc(added0, 1)
            groups(dve, add0)
            dve.wait_ge(added0, GR)
            norm(1)

            def add_si(n, k, first):
                dve.wait_ge(si_done, n + 1)
                nc.vector.tensor_tensor(group_columns(n), group_columns(n), fold_ps[0:NP, k, P:P + JG * D],
                                        ALU.add).then_inc(si_added, 1)
            groups(dve, add_si)

            STEPS = 6

            def products(n, r, q, meanwhile):
                def step(i):
                    dve.wait_ge(prod_step, n * STEPS + i)

                wts = wts_ps[q]
                s_in, v_in = z[:, r, :, 0:MUL], z[:, r, :, MUL:D]
                sh0, sh1 = sh_sb[:, r, :, 0:1], sh_sb[:, r, :, 1:4]
                nc.vector.tensor_tensor(vsh[:], v_in.rearrange("p g (i m) -> p g i m", m=3),
                                        sh1.unsqueeze(2).to_broadcast([P, G, MUL, 3]), ALU.mult).then_inc(prod_step, 1)
                nc.vector.tensor_tensor(coef[:, :, MUL:], z[:, r], sh0.to_broadcast([P, G, D]),
                                        ALU.mult).then_inc(prod_step, 1)
                meanwhile()
                step(1)
                nc.vector.tensor_reduce(coef[:, :, 0:MUL], vsh[:], AX, ALU.add).then_inc(prod_step, 1)
                dve.wait_ge(wts_ready, n + 1)
                nc.vector.tensor_tensor(p011[:], wts[:, :, 2 * BLK:3 * BLK].rearrange("p g (i o) -> p g i o", i=MUL),
                                        s_in.unsqueeze(3).to_broadcast([P, G, MUL, MUL]), ALU.mult).then_inc(prod_step, 1)
                step(2)
                coef_v = coef[:, :, 2 * MUL:].rearrange("p g (i m) -> p g i m", m=3)
                for m in range(3):
                    last = nc.vector.tensor_tensor(
                        p101[:, :, :, m * MUL:(m + 1) * MUL],
                        wts[:, :, 3 * BLK:].rearrange("p g (i o) -> p g i o", i=MUL),
                        coef_v[:, :, :, m:m + 1].to_broadcast([P, G, MUL, MUL]), ALU.mult)
                last.then_inc(prod_step, 1)
                step(3)
                nc.vector.tensor_tensor(
                    prod1[:, q], wts[:, :, 0:2 * BLK].rearrange("p g (i o) -> p g i o", o=MUL),
                    coef[:, :, 0:2 * MUL].unsqueeze(3).to_broadcast([P, G, 2 * MUL, MUL]),
                    ALU.mult).then_inc(wts_used, 1)
                step(4)
                nc.vector.tensor_reduce(t011[:], p011[:].rearrange("p g i o -> p g o i"), AX, ALU.add
                                        ).then_inc(prod_step, 1)
                step(5)
                nc.vector.tensor_tensor(prod2[:, q, :, 0:HV].rearrange("p g (i c) -> p g i c", i=MUL // 2),
                                        p101[:, :, 0:MUL // 2], p101[:, :, MUL // 2:], ALU.add)
                step(6)
                nc.vector.tensor_tensor(prod2[:, q, :, HV:HV + 3 * MUL].rearrange("p g (m o) -> p g m o", m=3),
                                        t011[:].unsqueeze(2).to_broadcast([P, G, 3, MUL]),
                                        sh1.unsqueeze(3).to_broadcast([P, G, 3, MUL]), ALU.mult).then_inc(msg1_ready, 1)

            def layer1(b, r, s):
                n = b * RING + r
                if s == 0:
                    dve.wait_ge(pads_set, 1)
                if s is None or s < S:
                    dve.wait_ge(z1_in[r], (b + 1) * 16 * G)
                    dve.wait_ge(sh_in[r], (b + 1) * 16)
                    products(n, r, r % 2, lambda: one_hots(n, r))
                if s is None or s >= 1:
                    if s == 1:
                        dve.wait_ge(cleared, 5)
                    take_sums(n - 1, None if s is None else s - 1, sum1_ready, acc1_done, P, 2)
            supertiles(dve, layer1, lag=1)

            def wide_messages1(n):
                dve.wait_ge(wide_in[1], (n + 1) * 48)
                products(n + S, 0, 0, lambda: None)
            wide_supertiles(1, wide_messages1, P, 2, acc1_done)

            def add1(n, k, first):
                dve.wait_ge(folded1, n + 1)
                nc.vector.tensor_tensor(group_columns(n), group_columns(n), fold_ps[0:NP, k, 0:JG * D],
                                        ALU.add).then_inc(added1, 1)
            groups(dve, add1)


def kernel(**inputs):
    import numpy as np
    import concourse.bacc as bacc
    from concourse.bass_utils import run_bass_kernel_spmd

    a = {k: np.ascontiguousarray(v) for k, v in inputs.items()}
    N, E = a["x"].shape[0], a["src"].shape[0]
    S = E // SUP
    assert S * SUP == E

    w1 = a["L1_gnn_W1"]
    w1_2 = np.zeros((P, P), w1.dtype)
    w1_2[:D, :HID], w1_2[D:2 * D, HID:] = w1, w1
    b1_2 = np.concatenate([a["L1_gnn_b1"], a["L1_gnn_b1"]])[:, None]
    w2 = np.concatenate([a["L1_gnn_W2"], a["L1_gnn_b2"][None]]).reshape(HID + 1, 4, BLK)
    w2_aug = np.zeros((P, WN), w2.dtype)
    w2_aug[:HID + 1] = w2[:, [3, 0, 1, 2]].reshape(HID + 1, WN)
    si_mat = np.zeros((JG, D, JG, D), w1.dtype)
    for j in range(JG):
        si_mat[j, :MUL, j, :MUL] = a["L1_gnn_si_w0"]
        for m in range(3):
            si_mat[j, MUL + m::3, j, MUL + m::3] = a["L1_gnn_si_w1"]

    alpha, c110 = 0.25, 3 ** -0.5
    sel = np.zeros((P, 3, D), np.float32)
    sel[:D, 0] = np.eye(D)
    for i in range(2 * MUL):
        for o in range(MUL):
            sel[i * MUL + o, 1, o] = alpha * (c110 if i < MUL else 1.0)
    for c in range(HV + 3 * MUL):
        m, o = divmod(c % (3 * MUL), MUL)
        sel[c, 2, MUL + 3 * o + m] = alpha

    arrays = {
        "x": a["x"],
        "src_t": a["src"].reshape(S, G, P).transpose(0, 2, 1),
        "src_flat": a["src"].reshape(S, 1, SUP),
        "dst_flat": a["dst"],
        "dst_t": a["dst"].reshape(S * G, P).T,
        "ew_t": a["edge_weight"].reshape(S, G, P).transpose(0, 2, 1),
        "sh_t": a["edge_attr_4"].reshape(S, G, P, 4).transpose(0, 2, 1, 3).reshape(S, P, G * 4),
        "ft": a["edge_attr_32"].reshape(S, 2, HALF, D).transpose(0, 1, 3, 2).reshape(S, 2 * D, HALF),
        "w1_2": w1_2, "b1_2": b1_2, "w2_aug": w2_aug, "si_mat": si_mat.reshape(JG * D, JG * D),
        "iota": np.tile(np.arange(WIN, dtype=np.float32), (P, 1)),
        "lane": np.arange(P, dtype=np.float32)[:, None],
        "blocks": np.tile(np.arange(GB, dtype=np.float32) * P, (P, 1)),
        "ident": np.eye(P, dtype=np.float32),
        "sel": sel,
    }
    nc = bacc.Bacc("TRN2", target_bir_lowering=False, num_devices=1)
    sent, args = {}, []
    for name, v in arrays.items():
        v = np.ascontiguousarray(v)
        sent[f"in_{name}"] = v
        args.append(nc.dram_tensor(f"in_{name}", v.shape, mybir.dt.from_np(v.dtype), kind="ExternalInput").ap())
    args.append(nc.dram_tensor("out_0", (N, D), F32, kind="ExternalOutput").ap())
    gnn_two_layers(nc, *args)
    r = run_bass_kernel_spmd(nc, [sent], core_ids=[0])
    return r.results[0]["out_0"]
```

```python
from contextlib import ExitStack

import concourse.bass as bass
from concourse import mybir

P = 128
G = 5
SUP = G * P
HALF = SUP // 2
WIN = 64
RING = 4
MUL = 8
D = 4 * MUL
HID = 64
BLK = MUL * MUL
WN = 4 * BLK
HV = (MUL // 2) * 3 * MUL
PEG = 3
GB = 8
JG = 4
EPS = 1e-5

F32 = mybir.dt.float32
BF16 = mybir.dt.bfloat16
I32 = mybir.dt.int32
ALU = mybir.AluOpType
ACT = mybir.ActivationFunctionType
AX = mybir.AxisListType.X


def largest_divisor(n, most):
    return max(k for k in range(1, most + 1) if n % k == 0)


def gnn_two_layers(nc, x, src_t, src_flat, dst_flat, dst_t, ew_t, sh_t, ft, w1_2, b1_2, w2_aug, si_mat, iota,
                   lane, blocks, ident, sel, out):
    N = x.shape[0]
    S = src_t.shape[0]
    T = S * G
    NP = largest_divisor(N, 125)
    J = N // NP
    GR = J // JG
    GU = largest_divisor(GR, 5)
    CH = GR // GU
    SPP = largest_divisor(S, 125)
    SK = S // SPP
    FULL = S // RING
    NWIN = -(-N // WIN)
    AW = NWIN * WIN + WIN
    NC = -(-N // (GB * P))
    KD = NC * GB * D
    assert NC * D <= 512
    assert J % JG == 0 and FULL >= 2 and GU >= 2

    def uses(r):
        return FULL + (1 if r < S % RING else 0)

    def pool_tiles(r):
        return G - 1 if r < PEG else G

    def before(b, r, k):
        return b + (r - k) // RING, (r - k) % RING

    with ExitStack() as ctx:
        def sb(name, shape, dt=F32):
            return ctx.enter_context(nc.sbuf_tensor(name, shape, dt))

        def psum(name, shape):
            return ctx.enter_context(nc.psum_tensor(name, shape, F32))

        def sem(name):
            return ctx.enter_context(nc.semaphore(name))

        def sems(name):
            return [sem(f"{name}{r}") for r in range(RING)]

        h0_dram = nc.dram_tensor("h0_table", [N, D], F32).ap()
        h1_dram = nc.dram_tensor("h1_table", [N, D], F32).ap()
        base_dram = nc.dram_tensor("base_table", [S], I32).ap()
        span_dram = nc.dram_tensor("span_table", [S], I32).ap()

        w_ps = psum("w_ps", [P, 2, 3, 512])
        hp_ps = psum("hp_ps", [P, 512])
        sc_ps = psum("sc_ps", [P, 512])
        wts_ps = [w_ps[:, q].rearrange("p k n -> p (k n)")[:, 0:G * WN].rearrange("p (g n) -> p g n", g=G)
                  for q in range(2)]
        sums_ps = sc_ps[:, 0:2 * WIN].rearrange("p (k n) -> p k n", k=2)
        total0_ps = sc_ps[0:D, 2 * WIN:3 * WIN]
        total1_ps = [w_ps[0:D, q, 2, 256:256 + WIN] for q in range(2)]
        fold_ps = w_ps[:].rearrange("p q k n -> p (q k) n")

        acc = sb("acc", [D, AW])
        x_sb = sb("x_sb", [NP, J * D])
        big = sb("big", [P, max(J * D, KD)])
        st_sum, st_neg, st_var = (sb(n, [NP, J]) for n in ("st_sum", "st_neg", "st_var"))
        st_eps, st_std, st_inv = (sb(n, [NP, J]) for n in ("st_eps", "st_std", "st_inv"))
        stage_flat = sb("stage", [P, max(GU * NP, 3 * KD // 2)])
        squares = sb("squares", [NP, J * D])
        stage = stage_flat[:, 0:GU * NP].rearrange("p (k n) -> p k n", k=GU)
        feat = sb("feat", [P, max(GU, PEG), JG * D])
        dst_sb = sb("dst_sb", [SPP, SK * SUP], I32)
        rel_sb = sb("rel_sb", [P, T])
        base_row, span_row = sb("base_row", [1, S], I32), sb("span_row", [1, S], I32)
        span_max = sb("span_max", [1, 1], I32)
        base_bc = sb("base_bc", [P, S], I32)
        least, most = sb("least", [SPP, SK]), sb("most", [SPP, SK])
        least_i, span_i = sb("least_i", [SPP, SK], I32), sb("span_i", [SPP, SK], I32)
        iota_sb = sb("iota_sb", [P, WIN])
        lane_sb, block_sb = sb("lane_sb", [P, 1]), sb("block_sb", [P, GB])
        wide_dst, wide_near = sb("wide_dst", [P, G]), sb("wide_near", [P, G])
        id_sb = sb("id_sb", [P, P])
        sel_sb = sb("sel_sb", [P, 2, D])
        sums_sb = sb("sums_sb", [P, 2, WIN])
        w1_sb = sb("w1_sb", [P, P])
        b1_sb = sb("b1_sb", [P, 1])
        w2_sb = sb("w2_sb", [P, WN])
        si_raw, si_sb = sb("si_raw", [JG * D, JG * D]), sb("si_sb", [JG * D, JG * D])
        idx = sb("idx", [P, RING, G], I32)
        ew_sb = sb("ew_sb", [P, RING, G])
        z = sb("z", [P, RING, G, D])
        onehot = sb("onehot", [P, RING, G, WIN])
        ft_sb = sb("ft_sb", [P, RING, HALF])
        sh_sb = sb("sh_sb", [P, RING, G, 4])
        hid = sb("hid", [P, 2, SUP])
        coef = sb("coef", [P, G, MUL + D])
        vsh = sb("vsh", [P, G, MUL, 3])
        p011 = sb("p011", [P, G, MUL, MUL])
        t011 = sb("t011", [P, G, MUL])
        p101 = sb("p101", [P, G, MUL, 3 * MUL])
        prod1 = sb("prod1", [P, 2, G, 2 * MUL, MUL])
        prod2 = sb("prod2", [P, 2, G, P])

        parts = stage_flat[:, 0:3 * KD // 2].bitcast(BF16).rearrange("p (t c b d) -> p t c b d", t=3, c=NC, b=GB)
        flat_parts = parts.rearrange("p t c b d -> p t (c b d)")
        table = big[:, 0:KD]
        table_halves = [slice(0, KD // 2), slice(KD // 2, KD)]
        pick = [t[:, 0:GB * P // 2].bitcast(BF16).rearrange("p (b e) -> p b e", b=GB) for t in (
            prod1[:, 0].rearrange("p g i o -> p (g i o)"), prod1[:, 1].rearrange("p g i o -> p (g i o)"),
            prod2[:, 0].rearrange("p g c -> p (g c)"))]
        group_prod = p101[:].rearrange("p g i c -> p (g i c)")[:, 0:NC * D].rearrange("p (c d) -> p c d", d=D)
        key_in, key = feat[:].bitcast(I32), feat
        group_id, group_hot = sb("group_id", [P, 1], I32), sb("group_hot", [P, NC])

        x_in, dst_in, dstt_in, const_in = (
            sem(n) for n in ("x_in", "dst_in", "dstt_in", "const_in"))
        reduced, table_ready, tab_out, tab_in, rel_ready = (
            sem(n) for n in ("reduced", "table_ready", "tab_out", "tab_in", "rel_ready"))
        cleared, ones_set, pads_set = sem("cleared"), sem("ones_set"), sem("pads_set")
        norm_step, var_step, var_ready, std_ready, h_ready, h_out = (
            sem(n) for n in ("norm_step", "var_step", "var_ready", "std_ready", "h_ready", "h_out"))
        act_staged, pool_staged, folded, added = ([sem(f"{n}{layer}") for layer in (0, 1)] for n in (
            "act_staged", "pool_staged", "folded", "added"))
        res_out = sem("res_out")
        si_scaled, feat_staged, turned, turned_copied, si_done, si_added = (
            sem(n) for n in ("si_scaled", "feat_staged", "turned", "turned_copied", "si_done", "si_added"))
        idx0_in, z0_in, ew_in = sems("idx0_in"), sems("z0_in"), sems("ew_in")
        msg0_ready, sum0_ready, acc0_done = sem("msg0_ready"), sem("sum0_ready"), sem("acc0_done")
        keys_in = [sem(f"keys_in{r}") for r in range(PEG)]
        table_padded, table_in, split_act, split_dve = (
            sem(n) for n in ("table_padded", "table_in", "split_act", "split_dve"))
        key_step, pick_ready, picked, group_step = (
            sem(n) for n in ("key_step", "pick_ready", "picked", "group_step"))
        idx1_in, z1_in, sh_in, ft_in = sems("idx1_in"), sems("z1_in"), sems("sh_in"), sems("ft_in")
        hidpre_ready, hid_ready, wts_ready, wts_used = (
            sem(n) for n in ("hidpre_ready", "hid_ready", "wts_ready", "wts_used"))
        prod_step, msg1_ready, sum1_ready, sum1_copied, total1_ready, acc1_done = (
            sem(n) for n in ("prod_step", "msg1_ready", "sum1_ready", "sum1_copied", "total1_ready", "acc1_done"))

        def supertiles(eng, body, lag=0):
            for s in range(RING):
                body(0, s, s)
            with eng.Fori(1, FULL) as b:
                for r in range(RING):
                    body(b, r, None)
            for s in range(FULL * RING, S + lag):
                body(s // RING, s % RING, s)

        def groups(eng, body):
            for k in range(GU):
                body(k, k, True, 0)
            if GR > GU:
                with eng.Fori(1, GR // GU) as g:
                    for k in range(GU):
                        body(g * GU + k, k, False, g)

        assert JG * D == P and G == 5 and 4 * WN == 1024

        def stage_columns(op, n, k, js, staged):
            for j in js:
                col = acc[:, 0:N].rearrange("r (p j) -> r j p", p=NP)[:, bass.ds(n * JG + j, 1), :]
                last = op(stage[j * D:(j + 1) * D, k:k + 1], col)
            last.then_inc(staged, 1)

        span_ready = sem("span_ready")
        wide_free, wide_in, wide_z = ([sem(f"{n}{layer}") for layer in (0, 1)] for n in ("wide_free", "wide_in", "wide_z"))
        wide_step, wide_hot, wide_sum = ([sem(f"{n}{layer}") for layer in (0, 1)] for n in ("wide_step", "wide_hot", "wide_sum"))
        wide_added = [sem("wide_added0"), sem("wide_added1")]
        wide_partial, wide_copied = sem("wide_partial"), sem("wide_copied")

        def if_wide(eng):
            eng.wait_ge(span_ready, 1)
            return eng.If(eng.value_load(span_max[0:1, 0:1], min_val=0, max_val=N - 1) >= WIN)

        block = ctx.enter_context(nc.Block())

        @block.sync
        def _(sp):
            sp.dma_start(x_sb[:], x.rearrange("(p j) d -> p (j d)", p=NP)).then_inc(x_in, 16)
            sp.dma_start(dst_sb[:],
                         dst_flat.rearrange("(p e) -> p e", p=SPP)).then_inc(dst_in, 16)
            sp.dma_start(rel_sb[:].bitcast(I32), dst_t).then_inc(dstt_in, 16)
            for to, of in ((iota_sb, iota), (lane_sb, lane), (block_sb, blocks), (id_sb, ident), (sel_sb, sel), (w1_sb, w1_2), (b1_sb, b1_2),
                           (w2_sb, w2_aug), (si_raw, si_mat)):
                sp.dma_start(to[:], of).then_inc(const_in, 16)
            def store_features(turn, dram):
                for c in range(CH):
                    sp.wait_ge(h_ready, turn * CH + c + 1)
                    cols = slice(c * J // CH * D, (c + 1) * J // CH * D)
                    sp.dma_start(dram.rearrange("(p j) d -> p (j d)", p=NP)[:, cols], big[0:NP, cols]).then_inc(h_out, 16)
            store_features(0, h0_dram)

            def load_tables():
                whole = N // P
                cuts = [q * whole // 4 for q in range(5)]

                def load_piece(q):
                    sp.dma_start(table[:, cuts[q] * D:cuts[q + 1] * D].rearrange("a (k d) -> a k d", d=D),
                                 h0_dram[cuts[q] * P:cuts[q + 1] * P].rearrange("(k a) d -> a k d", a=P)
                                 ).then_inc(table_in, 16)
                sp.wait_ge(h_out, 16 * CH)
                sp.wait_ge(table_padded, 1)
                if whole * P < N:
                    sp.dma_start(table[0:N - whole * P, whole * D:(whole + 1) * D], h0_dram[whole * P:N]
                                 ).then_inc(table_in, 16)
                load_piece(0)
                load_piece(1)
                sp.wait_ge(table_ready, 2)
                sp.dma_start(base_dram.rearrange("(p k) -> p k", p=SPP), least_i[:]).then_inc(tab_out, 16)
                sp.dma_start(span_dram.rearrange("(p k) -> p k", p=SPP), span_i[:]).then_inc(tab_out, 16)
                load_piece(2)
                sp.wait_ge(tab_out, 32)
                sp.dma_start(base_row[:], base_dram.rearrange("(a s) -> a s", a=1)).then_inc(tab_in, 16)
                sp.dma_start(span_row[:], span_dram.rearrange("(a s) -> a s", a=1)).then_inc(tab_in, 16)
                sp.dma_start(base_bc[:], base_dram.rearrange("(a s) -> a s", a=1).to_broadcast([P, S])
                             ).then_inc(tab_in, 16)
                load_piece(3)

            def load0(b, r, s):
                n = b * RING + r
                if s is None or s >= RING:
                    sp.wait_ge(z0_in[r], b * 16 * pool_tiles(r))
                    sp.nop(nofuse=True)
                    sp.wait_ge(msg0_ready, n - RING + 1)
                    sp.nop(nofuse=True)
                sp.dma_start(idx[:, r, :], src_t[n]).then_inc(idx0_in[r], 16)
                sp.dma_start(ew_sb[:, r, :], ew_t[n]).then_inc(ew_in[r], 16)
                if r < PEG:
                    sp.dma_start(key_in[:, r, :], src_flat[n, :, (G - 1) * P:G * P].to_broadcast([P, P])
                                 ).then_inc(keys_in[r], 16)
                if s == RING - 1:
                    load_tables()
            supertiles(sp, load0)

            def wide_loads(layer, loads):
                with if_wide(sp):
                    with sp.Fori(0, S) as n:
                        sp.wait_ge(wide_free[layer], n + 1)
                        for to, of in loads:
                            sp.dma_start(to, of[n]).then_inc(wide_in[layer], 16)
                    sp.wait_ge(wide_free[layer], S + 1)
            wide_loads(0, [(idx[:, 0, :], src_t), (ew_sb[:, 0, :], ew_t)])

            store_features(1, h1_dram)

            def load1(b, r, s):
                n = b * RING + r
                if s is not None and s < RING:
                    sp.wait_ge(z0_in[r], uses(r) * 16 * pool_tiles(r))
                else:
                    sp.wait_ge(z1_in[r], b * 16 * G)
                sp.dma_start(idx[:, r, :], src_t[n]).then_inc(idx1_in[r], 16)
                if s is None or s >= RING:
                    sp.wait_ge(hidpre_ready, n - RING + 1)
                sp.dma_start(ft_sb[0:2 * D, r, :], ft[n]).then_inc(ft_in[r], 16)
                if s is None or s >= RING:
                    sp.wait_ge(msg1_ready, n - RING + 1)
                sp.dma_start(sh_sb[:, r].rearrange("p g c -> p (g c)"), sh_t[n]).then_inc(sh_in[r], 16)
            supertiles(sp, load1)
            wide_loads(1, [(idx[:, 0, :], src_t), (ft_sb[0:2 * D, 0, :], ft), (sh_sb[:, 0].rearrange("p g c -> p (g c)"), sh_t)])

            sp.wait_ge(added[1], GR)
            sp.dma_start(out.rearrange("(p j) d -> p (j d)", p=NP), x_sb[:]).then_inc(res_out, 16)
            sp.wait_ge(res_out, 16)

        @block.gpsimd
        def _(pool):
            pool.memset(acc[:], 0.0).then_inc(cleared, 1)
            pool.wait_ge(cleared, 1)
            pool.memset(ft_sb[2 * D:], 0.0).then_inc(cleared, 1)
            pool.wait_ge(cleared, 2)
            pool.memset(hid[HID:], 0.0).then_inc(cleared, 1)
            pool.wait_ge(cleared, 3)
            pool.memset(hid[HID:HID + 1], 1.0).then_inc(ones_set, 1)

            def gathers(rows, idx_in, z_in, used, tiles):
                def gather(b, r, s):
                    n = b * RING + r
                    pool.wait_ge(idx_in[r], (b + 1) * 16)
                    if s is None or s >= RING:
                        pool.nop(nofuse=True)
                        pool.wait_ge(used, n - RING + 1)
                    pool.nop(nofuse=True)
                    for u in range(tiles(r)):
                        pool.indirect_dma_start(
                            z[:, r, u, :], None, rows,
                            bass.IndirectOffsetOnAxis(ap=idx[:, r, u:u + 1], axis=0)).then_inc(z_in[r], 16)
                return gather

            pool.wait_ge(ones_set, 1)
            pool.nop(nofuse=True)
            pool.wait_ge(h_out, 16 * CH)
            pool.memset(table[:, N // P * D:KD], 0.0).then_inc(table_padded, 1)
            supertiles(pool, gathers(h0_dram, idx0_in, z0_in, sum0_ready, pool_tiles))

            def wide_gathers(layer, rows, loads):
                with if_wide(pool):
                    with pool.Fori(0, S) as n:
                        pool.wait_ge(wide_in[layer], (n + 1) * 16 * loads)
                        pool.nop(nofuse=True)
                        for u in range(G):
                            pool.indirect_dma_start(
                                z[:, 0, u, :], None, rows,
                                bass.IndirectOffsetOnAxis(ap=idx[:, 0, u:u + 1], axis=0)).then_inc(wide_z[layer], 16)
            wide_gathers(0, h0_dram, 2)

            def pool_stages(layer):
                pool.wait_ge((acc0_done, acc1_done)[layer], S)
                with if_wide(pool):
                    pool.wait_ge(wide_free[layer], S + 1)

                def stage_share(n, k, first, g):
                    if not first:
                        pool.wait_ge(folded[layer], n - GU + 1)
                        pool.nop(nofuse=True)
                    stage_columns(pool.tensor_copy, n, k, (3,), pool_staged[layer])
                groups(pool, stage_share)
            pool_stages(0)
            pool.wait_ge(folded[0], GR)
            pool.memset(prod2[:, :, :, HV + 3 * MUL:P], 0.0).then_inc(pads_set, 1)
            pool.wait_ge(pads_set, 1)
            pool.memset(acc[:], 0.0).then_inc(cleared, 1)
            pool.wait_ge(h_out, 32 * CH)
            pool.nop(nofuse=True)
            supertiles(pool, gathers(h1_dram, idx1_in, z1_in, msg1_ready, lambda r: G))
            wide_gathers(1, h1_dram, 3)
            pool_stages(1)

        @block.scalar
        def _(act):
            act.wait_ge(var_ready, 1)
            nc.scalar.activation(st_std[:], st_eps[:], ACT.Sqrt).then_inc(std_ready, 1)
            act.wait_ge(const_in, 16 * 9)
            nc.scalar.activation(si_sb[:], si_raw[:], ACT.Copy, scale=MUL ** -0.5).then_inc(si_scaled, 1)

            act.wait_ge(table_in, 16 * (4 + (N % P > 0)))
            for t in range(2):
                for h, half in enumerate(table_halves):
                    if t > 0:
                        act.wait_ge(split_dve, h + 1)
                    nc.scalar.activation(flat_parts[:, t, half], table[:, half], ACT.Copy).then_inc(split_act, 1)

            act.wait_ge(acc0_done, S)
            with if_wide(act):
                act.wait_ge(wide_free[0], S + 1)

            def act_stages(staged, folded):
                def stage_share(n, k, first, g):
                    if not first:
                        act.wait_ge(folded, n - GU + 1)
                        act.nop(nofuse=True)
                    stage_columns(lambda to, of: nc.scalar.activation(to, of, ACT.Copy), n, k, (0, 1, 2), staged)
                groups(act, stage_share)
            act_stages(act_staged[0], folded[0])

            act.wait_ge(var_ready, 2)
            nc.scalar.activation(st_std[:], st_eps[:], ACT.Sqrt).then_inc(std_ready, 1)
            def stage_feat(n, k, first, g):
                if k == 0:
                    act.wait_ge(h_ready, g + CH + 1)
                    if not first:
                        act.nop(nofuse=True)
                if not first:
                    act.wait_ge(turned, n - GU + 1)
                    act.nop(nofuse=True)
                nc.scalar.activation(feat[0:NP, k], big[0:NP, bass.ds(n * JG * D, JG * D)], ACT.Copy
                                     ).then_inc(feat_staged, 1)

            def copy_turned(n, k):
                act.wait_ge(turned, n + 1)
                nc.scalar.activation(stage[:, k], fold_ps[:, k, 0:NP], ACT.Copy
                                     ).then_inc(turned_copied, 1)

            def si_copies(n, k, first, g):
                stage_feat(n, k, first, g)
                if not first or k >= 1:
                    copy_turned(n - 1, (k - 1) % GU)
            groups(act, si_copies)
            copy_turned(GR - 1, GU - 1)

            def relu_halves(q):
                nc.scalar.activation(hid[0:HID, q, 0:HALF], hp_ps[0:HID, 0:HALF], ACT.Relu, bias=b1_sb[0:HID])
                nc.scalar.activation(hid[0:HID, q, HALF:SUP], hp_ps[HID:P, 0:HALF], ACT.Relu,
                                     bias=b1_sb[HID:P]).then_inc(hid_ready, 1)

            def copy_sums():
                return nc.scalar.activation(sums_sb[:], sums_ps, ACT.Copy)

            def relu(b, r, s):
                n = b * RING + r
                if s is None or s >= 3:
                    act.wait_ge(sum1_ready, n - 2)
                    copy_sums().then_inc(sum1_copied, 1)
                if s is not None and s >= S:
                    return
                if s == 0:
                    act.wait_ge(ones_set, 1)
                act.wait_ge(hidpre_ready, n + 1)
                if s is None or s >= 2:
                    act.wait_ge(wts_ready, n - 1)
                relu_halves(r % 2)
            supertiles(act, relu, lag=3)

            act.wait_ge(acc1_done, S)
            with if_wide(act):
                with act.Fori(0, S) as n:
                    act.wait_ge(hidpre_ready, n + S + 1)
                    act.nop(nofuse=True)
                    relu_halves(0)
                    with act.Fori(0, NWIN) as w:
                        act.wait_ge(wide_partial, n * NWIN + w + 1)
                        act.nop(nofuse=True)
                        copy_sums().then_inc(wide_copied, 1)
                act.wait_ge(wide_free[1], S + 1)

            act_stages(act_staged[1], folded[1])

        @block.tensor
        def _(pe):
            def sum0(b, r, s):
                n = b * RING + r
                if s == 0:
                    pe.wait_ge(split_dve, 4)
                if r < PEG and (s is None or s < S):
                    pe.wait_ge(pick_ready, b * PEG + r + 1)
                    for blk in range(GB):
                        for t in range(3):
                            mm = pe.matmul(fold_ps[:, r, 0:NC * D], pick[r][:, blk, :], parts[:, t, :, blk, :],
                                           start=(blk == 0 and t == 0), stop=(blk == GB - 1 and t == 2))
                    mm.then_inc(picked, 1)
                if s is None or s >= 2:
                    v = (r - 2) % RING
                    pe.wait_ge(msg0_ready, n - 1)
                    if s is None or s >= 3:
                        pe.wait_ge(acc0_done, n - 2)
                    for u in range(G):
                        mm = pe.matmul(total0_ps, z[:, v, u, :], onehot[:, v, u, :],
                                       start=(u == 0), stop=(u == G - 1))
                    mm.then_inc(sum0_ready, 1)
            supertiles(pe, sum0, lag=2)

            def wide_sums(layer, before, sums):
                with if_wide(pe):
                    with pe.Fori(0, S) as n:
                        before(n)
                        with pe.Fori(0, NWIN) as w:
                            pe.wait_ge(wide_hot[layer], n * NWIN + w + 1)
                            pe.nop(nofuse=True)
                            sums(n * NWIN + w).then_inc(wide_sum[layer], 1)

            def wide_sums0(turn):
                for u in range(G):
                    mm = pe.matmul(total0_ps, z[:, 0, u, :], onehot[:, 0, u, :],
                                   start=(u == 0), stop=(u == G - 1))
                return mm
            wide_sums(0, lambda n: None, wide_sums0)

            pe.wait_ge(const_in, 16 * 9)

            def folds(layer):
                def fold(n, k, first, g):
                    pe.wait_ge(act_staged[layer], n + 1)
                    pe.wait_ge(pool_staged[layer], n + 1)
                    if not first:
                        pe.wait_ge(added[layer], n - GU + 1)
                    pe.matmul(fold_ps[0:NP, k, 0:P], stage[:, k], id_sb[:], start=True, stop=True
                              ).then_inc(folded[layer], 1)
                groups(pe, fold)
            folds(0)

            pe.wait_ge(si_scaled, 1)
            pe.wait_ge(ones_set, 1)

            def self_interaction(n, k):
                pe.wait_ge(turned_copied, n + 1)
                pe.matmul(fold_ps[0:NP, k, P:2 * P], stage[:, k], si_sb[:],
                          start=True, stop=True).then_inc(si_done, 1)

            def turn(n, k, first, g):
                pe.wait_ge(feat_staged, n + 1)
                if first:
                    pe.wait_ge(added[0], GR)
                else:
                    pe.wait_ge(si_added, n - GU + 1)
                pe.transpose(fold_ps[:, k, 0:NP], feat[0:NP, k], id_sb[0:NP, 0:NP]).then_inc(turned, 1)
                if not first or k >= 1:
                    self_interaction(n - 1, (k - 1) % GU)
            groups(pe, turn)
            self_interaction(GR - 1, GU - 1)

            def hidden(r):
                return pe.matmul(hp_ps[:, 0:HALF], w1_sb[:], ft_sb[:, r, :], start=True, stop=True)

            def weights(q, meanwhile=lambda: None):
                for u in (4, 0, 1, 2, 3):
                    if u == 3:
                        meanwhile()
                    mm = pe.matmul(wts_ps[q][:, u, :], hid[:, q, u * P:(u + 1) * P], w2_sb[:],
                                   start=True, stop=True)
                return mm

            def window_sums(r):
                for u in range(G):
                    pe.matmul(sums_ps[:, 0, :], prod1[:, r % 2, u].rearrange("p i o -> p (i o)"),
                              onehot[:, r, u, :], start=(u == 0), stop=(u == G - 1))
                for u in range(G):
                    mm = pe.matmul(sums_ps[:, 1, :], prod2[:, r % 2, u, :], onehot[:, r, u, :],
                                   start=(u == 0), stop=(u == G - 1))
                return mm

            def product_sums(q):
                for blk in range(2):
                    mm = pe.matmul(total1_ps[q], sel_sb[:, blk, :], sums_sb[:, blk, :], start=(blk == 0), stop=(blk == 1))
                return mm

            def edge_layer(b, r, s):
                n = b * RING + r
                if s is None or s >= 3:
                    v = (r - 3) % RING
                    pe.wait_ge(msg1_ready, n - 2)
                    window_sums(v).then_inc(sum1_ready, 1)

                def totals():
                    if s is None or s >= 3:
                        pe.wait_ge(sum1_copied, n - 2)
                        if s is None or s >= 4:
                            pe.wait_ge(acc1_done, n - 3)
                        product_sums((r - 3) % 2).then_inc(total1_ready, 1)
                if s is None or 1 <= s <= S:
                    q = (r - 1) % 2
                    if s == 1:
                        pe.wait_ge(si_added, GR)
                    pe.wait_ge(hid_ready, n)
                    if s is None or s >= 3:
                        pe.wait_ge(wts_used, n - 2)
                    weights(q, totals).then_inc(wts_ready, 1)
                else:
                    totals()
                if s is None or s < S:
                    pe.wait_ge(ft_in[r], (b + 1) * 16)
                    if s is None or s >= 1:
                        pe.wait_ge(hid_ready, n)
                    hidden(r).then_inc(hidpre_ready, 1)
            supertiles(pe, edge_layer, lag=3)

            def wide_weights(n):
                pe.wait_ge(wide_in[1], (n + 1) * 48)
                pe.nop(nofuse=True)
                hidden(0).then_inc(hidpre_ready, 1)
                pe.wait_ge(hid_ready, n + S + 1)
                pe.nop(nofuse=True)
                weights(0).then_inc(wts_ready, 1)

            def wide_sums1(turn):
                window_sums(0).then_inc(wide_partial, 1)
                pe.wait_ge(wide_copied, turn + 1)
                pe.nop(nofuse=True)
                return product_sums(1)
            wide_sums(1, wide_weights, wide_sums1)

            folds(1)

        @block.vector
        def _(dve):
            def view(t):
                return t[0:NP, 0:J * D].rearrange("p (j d) -> p j d", d=D)

            def centre(first, count, step, ready, at):
                def columns(t):
                    return view(t)[:, bass.ds(first, count), :]

                def column_stats(t):
                    return t[:, bass.ds(first, count)]
                dve.wait_ge(ready, at)
                nc.vector.tensor_reduce(column_stats(st_sum), columns(x_sb), AX, ALU.add).then_inc(norm_step, 1)
                dve.wait_ge(norm_step, step + 1)
                nc.vector.tensor_scalar(column_stats(st_neg), column_stats(st_sum), -1.0 / D, None, ALU.mult
                                        ).then_inc(norm_step, 1)
                dve.wait_ge(norm_step, step + 2)
                nc.vector.tensor_tensor(columns(big), columns(x_sb),
                                        column_stats(st_neg).unsqueeze(2).to_broadcast([NP, count, D]),
                                        ALU.add).then_inc(norm_step, 1)
                dve.wait_ge(norm_step, step + 3)
                nc.vector.tensor_tensor(columns(squares), columns(big), columns(big), ALU.mult).then_inc(norm_step, 1)

            def normalise(turn, step):
                dve.wait_ge(norm_step, step)
                nc.vector.tensor_reduce(st_var[:], view(squares), AX, ALU.add).then_inc(var_step, 1)
                dve.wait_ge(var_step, turn * 2 + 1)
                nc.vector.tensor_scalar(st_eps[:], st_var[:], 1.0 / D, EPS, ALU.mult, ALU.add).then_inc(var_ready, 1)
                dve.wait_ge(std_ready, 1 + turn)
                nc.vector.reciprocal(st_inv[:], st_std[:]).then_inc(var_step, 1)
                dve.wait_ge(var_step, turn * 2 + 2)
                for c in range(CH):
                    cols = slice(c * J // CH, (c + 1) * J // CH)
                    nc.vector.scalar_tensor_tensor(
                        view(big)[:, cols], view(big)[:, cols], 0.0,
                        st_inv[:, cols].unsqueeze(2).to_broadcast([NP, J // CH, D]),
                        ALU.max, ALU.mult).then_inc(h_ready, 1)

            centre(0, J, 0, x_in, 16)
            normalise(0, 4)

            dve.wait_ge(dst_in, 16)
            dst_s = dst_sb[:].rearrange("p (k e) -> p k e", k=SK)
            nc.vector.tensor_reduce(least[:], dst_s, AX, ALU.min).then_inc(reduced, 1)
            nc.vector.tensor_reduce(most[:], dst_s, AX, ALU.max).then_inc(reduced, 1)
            dve.wait_ge(reduced, 2)
            nc.vector.tensor_copy(least_i[:], least[:]).then_inc(table_ready, 1)
            nc.vector.tensor_tensor(span_i[:], most[:], least[:], ALU.subtract).then_inc(table_ready, 1)

            dve.wait_ge(dstt_in, 16)
            dve.wait_ge(tab_in, 48)
            nc.vector.tensor_tensor(rel_sb[:].rearrange("p (s g) -> p s g", g=G),
                                    rel_sb[:].bitcast(I32).rearrange("p (s g) -> p s g", g=G),
                                    base_bc[:].unsqueeze(2).to_broadcast([P, S, G]),
                                    ALU.subtract).then_inc(rel_ready, 1)
            nc.vector.tensor_reduce(span_max[:], span_row[:], AX, ALU.max).then_inc(span_ready, 1)
            dve.wait_ge(rel_ready, 1)
            dve.wait_ge(const_in, 16 * 9)

            for t in range(2):
                for h, half in enumerate(table_halves):
                    dve.wait_ge(split_act, t * 2 + h + 1)
                    rest = flat_parts[:, 2, half] if t else table[:, half]
                    nc.vector.tensor_tensor(rest, table[:, half], flat_parts[:, t, half], ALU.subtract
                                            ).then_inc(split_dve, 1)

            def tile_columns(t, n):
                return t[:, bass.ds(n * G, G)]

            def one_hots(n, r):
                return nc.vector.tensor_tensor(
                    onehot[:, r], iota_sb[:].unsqueeze(1).to_broadcast([P, G, WIN]),
                    tile_columns(rel_sb, n).unsqueeze(2).to_broadcast([P, G, WIN]), ALU.is_equal)

            def take_sums(n, s, ready, done, total_ps):
                base = dve.value_load(base_row[0:1, bass.ds(n, 1)], min_val=0, max_val=N - 1)
                dve.wait_ge(ready, n + 1)
                if s is None or s >= 1:
                    dve.wait_ge(done, n)
                at = acc[:, bass.ds(base, WIN)]
                nc.vector.tensor_tensor(at, at, total_ps, ALU.add).then_inc(done, 1)

            def make_pick(b, r, s):
                done = b * PEG + r
                dve.wait_ge(keys_in[r], (b + 1) * 16)
                nc.vector.tensor_scalar(key_in[:, r], key_in[:, r], GB * P - 1, None, ALU.bitwise_and
                                        ).then_inc(key_step, 1)
                dve.wait_ge(key_step, done * 2 + 1)
                nc.vector.tensor_scalar(key[:, r], key_in[:, r], lane_sb[:], None, ALU.subtract).then_inc(key_step, 1)
                dve.wait_ge(key_step, done * 2 + 2)
                if s is None or s >= RING:
                    dve.wait_ge(picked, b * PEG + r - PEG + 1)
                nc.vector.tensor_tensor(pick[r], key[:, r].unsqueeze(1).to_broadcast([P, GB, P]),
                                        block_sb[:].unsqueeze(2).to_broadcast([P, GB, P]), ALU.is_equal
                                        ).then_inc(pick_ready, 1)

            def select_group(b, r):
                done = (b * PEG + r) * 4
                dve.wait_ge(idx0_in[r], (b + 1) * 16)
                nc.vector.tensor_scalar(group_id[:], idx[:, r, G - 1:G], (GB * P).bit_length() - 1, None,
                                        ALU.logical_shift_right).then_inc(group_step, 1)
                dve.wait_ge(group_step, done + 1)
                nc.vector.tensor_tensor(group_hot[:], iota_sb[:, 0:NC], group_id[:].to_broadcast([P, NC]),
                                        ALU.is_equal).then_inc(group_step, 1)
                dve.wait_ge(group_step, done + 2)
                dve.wait_ge(picked, b * PEG + r + 1)
                nc.vector.tensor_tensor(group_prod, fold_ps[:, r, 0:NC * D].rearrange("p (c d) -> p c d", d=D),
                                        group_hot[:].unsqueeze(2).to_broadcast([P, NC, D]), ALU.mult
                                        ).then_inc(group_step, 1)
                dve.wait_ge(group_step, done + 3)
                nc.vector.tensor_reduce(z[:, r, G - 1, :], group_prod.rearrange("p c d -> p d c"), AX, ALU.add
                                        ).then_inc(group_step, 1)
                dve.wait_ge(group_step, done + 4)

            def layer0(b, r, s):
                n = b * RING + r
                if r < PEG and (s is None or s < S):
                    make_pick(b, r, s)
                if s is None or 2 <= s <= S + 1:
                    bv, v = before(b, r, 2)
                    one_hots(n - 2, v)
                    if v < PEG:
                        select_group(bv, v)
                    dve.wait_ge(z0_in[v], (bv + 1) * 16 * pool_tiles(v))
                    dve.wait_ge(ew_in[v], (bv + 1) * 16)
                    nc.vector.tensor_tensor(z[:, v], z[:, v], ew_sb[:, v].unsqueeze(2).to_broadcast([P, G, D]),
                                            ALU.mult).then_inc(msg0_ready, 1)
                if s is None or s >= 3:
                    if s == 3:
                        dve.wait_ge(cleared, 1)
                    take_sums(n - 3, None if s is None else s - 3, sum0_ready, acc0_done, total0_ps)
            supertiles(dve, layer0, lag=3)

            def wide_supertiles(layer, before, last_add, total_ps):
                free, stepped, hot, summed = wide_free[layer], wide_step[layer], wide_hot[layer], wide_sum[layer]
                added = wide_added[layer]
                with if_wide(dve):
                    dve.wait_ge(last_add, S)
                    dve.nop(nofuse=True)
                    dve.engine_nop().then_inc(free, 1)
                    with dve.Fori(0, S) as n:
                        dve.wait_ge(wide_z[layer], (n + 1) * 16 * G)
                        dve.nop(nofuse=True)
                        before(n)
                        rel = tile_columns(rel_sb, n)
                        nc.vector.tensor_scalar(wide_near[:], rel, float(WIN), float(2 * AW), ALU.is_lt, ALU.mult
                                                ).then_inc(stepped, 1)
                        nc.vector.tensor_tensor(wide_dst[:], rel, base_bc[:, bass.ds(n, 1)].to_broadcast([P, G]),
                                                ALU.add).then_inc(stepped, 1)
                        dve.wait_ge(stepped, n * 3 + 2)
                        nc.vector.tensor_tensor(wide_dst[:], wide_dst[:], wide_near[:], ALU.add).then_inc(stepped, 1)
                        dve.wait_ge(stepped, n * 3 + 3)
                        dve.nop(nofuse=True)
                        with dve.Fori(0, NWIN) as w:
                            turn = n * NWIN + w
                            nc.vector.tensor_tensor(
                                onehot[:, 0], iota_sb[:].unsqueeze(1).to_broadcast([P, G, WIN]),
                                wide_dst[:].unsqueeze(2).to_broadcast([P, G, WIN]), ALU.is_equal).then_inc(hot, 1)
                            dve.wait_ge(summed, turn + 1)
                            dve.nop(nofuse=True)
                            nc.vector.tensor_scalar(wide_dst[:], wide_dst[:], float(-WIN), None, ALU.add
                                                    ).then_inc(added, 1)
                            at = acc[:, bass.ds(w * WIN, WIN)]
                            nc.vector.tensor_tensor(at, at, total_ps, ALU.add).then_inc(added, 1)
                            dve.wait_ge(added, turn * 2 + 2)
                            dve.nop(nofuse=True)
                        dve.engine_nop().then_inc(free, 1)

            def wide_messages0(n):
                dve.wait_ge(wide_in[0], (n + 1) * 32)
                nc.vector.tensor_tensor(z[:, 0], z[:, 0], ew_sb[:, 0].unsqueeze(2).to_broadcast([P, G, D]),
                                        ALU.mult)
            wide_supertiles(0, wide_messages0, acc0_done, total0_ps)

            def group_columns(n):
                return x_sb[:, bass.ds(n * JG * D, JG * D)]

            def add_folded(layer, n, k):
                dve.wait_ge(folded[layer], n + 1)
                nc.vector.tensor_tensor(group_columns(n), group_columns(n), fold_ps[0:NP, k, 0:JG * D],
                                        ALU.add).then_inc(added[layer], 1)

            def add0(n, k, first, g):
                add_folded(0, n, k)
                if k == GU - 1:
                    centre(g * (GU * JG), GU * JG, g * 4 + 4, added[0], n + 1)
            groups(dve, add0)
            normalise(1, 4 * (1 + CH))

            def add_si(n, k, first, g):
                dve.wait_ge(si_done, n + 1)
                nc.vector.tensor_tensor(group_columns(n), group_columns(n), fold_ps[0:NP, k, P:P + JG * D],
                                        ALU.add).then_inc(si_added, 1)
            groups(dve, add_si)

            STEPS = 6

            def products(n, r, q, meanwhile):
                def step(i):
                    dve.wait_ge(prod_step, n * STEPS + i)

                wts = wts_ps[q]
                s_in, v_in = z[:, r, :, 0:MUL], z[:, r, :, MUL:D]
                sh0, sh1 = sh_sb[:, r, :, 0:1], sh_sb[:, r, :, 1:4]
                nc.vector.tensor_tensor(vsh[:], v_in.rearrange("p g (i m) -> p g i m", m=3),
                                        sh1.unsqueeze(2).to_broadcast([P, G, MUL, 3]), ALU.mult).then_inc(prod_step, 1)
                nc.vector.tensor_tensor(coef[:, :, MUL:], z[:, r], sh0.to_broadcast([P, G, D]),
                                        ALU.mult).then_inc(prod_step, 1)
                meanwhile()
                step(1)
                nc.vector.tensor_reduce(coef[:, :, 0:MUL], vsh[:], AX, ALU.add).then_inc(prod_step, 1)
                dve.wait_ge(wts_ready, n + 1)
                nc.vector.tensor_tensor(p011[:], wts[:, :, 2 * BLK:3 * BLK].rearrange("p g (i o) -> p g i o", i=MUL),
                                        s_in.unsqueeze(3).to_broadcast([P, G, MUL, MUL]), ALU.mult).then_inc(prod_step, 1)
                step(2)
                coef_v = coef[:, :, 2 * MUL:].rearrange("p g (i m) -> p g i m", m=3)
                for m in range(3):
                    last = nc.vector.tensor_tensor(
                        p101[:, :, :, m * MUL:(m + 1) * MUL],
                        wts[:, :, 3 * BLK:].rearrange("p g (i o) -> p g i o", i=MUL),
                        coef_v[:, :, :, m:m + 1].to_broadcast([P, G, MUL, MUL]), ALU.mult)
                last.then_inc(prod_step, 1)
                step(3)
                nc.vector.tensor_tensor(
                    prod1[:, q], wts[:, :, 0:2 * BLK].rearrange("p g (i o) -> p g i o", o=MUL),
                    coef[:, :, 0:2 * MUL].unsqueeze(3).to_broadcast([P, G, 2 * MUL, MUL]),
                    ALU.mult).then_inc(wts_used, 1)
                step(4)
                nc.vector.tensor_reduce(t011[:], p011[:].rearrange("p g i o -> p g o i"), AX, ALU.add
                                        ).then_inc(prod_step, 1)
                step(5)
                nc.vector.tensor_tensor(prod2[:, q, :, 0:HV].rearrange("p g (i c) -> p g i c", i=MUL // 2),
                                        p101[:, :, 0:MUL // 2], p101[:, :, MUL // 2:], ALU.add)
                step(6)
                nc.vector.tensor_tensor(prod2[:, q, :, HV:HV + 3 * MUL].rearrange("p g (m o) -> p g m o", m=3),
                                        t011[:].unsqueeze(2).to_broadcast([P, G, 3, MUL]),
                                        sh1.unsqueeze(3).to_broadcast([P, G, 3, MUL]), ALU.mult).then_inc(msg1_ready, 1)

            def layer1(b, r, s):
                n = b * RING + r
                if s == 0:
                    dve.wait_ge(pads_set, 1)
                if s is None or s < S:
                    dve.wait_ge(z1_in[r], (b + 1) * 16 * G)
                    dve.wait_ge(sh_in[r], (b + 1) * 16)
                    products(n, r, r % 2, lambda: one_hots(n, r))
                if s is None or s >= 1:
                    if s == 1:
                        dve.wait_ge(cleared, 4)
                    take_sums(n - 1, None if s is None else s - 1, total1_ready, acc1_done, total1_ps[(r - 1) % 2])
            supertiles(dve, layer1, lag=1)

            def wide_messages1(n):
                dve.wait_ge(wide_in[1], (n + 1) * 48)
                products(n + S, 0, 0, lambda: None)
            wide_supertiles(1, wide_messages1, acc1_done, total1_ps[1])

            groups(dve, lambda n, k, first, g: add_folded(1, n, k))


def kernel(**inputs):
    import numpy as np
    import concourse.bacc as bacc
    from concourse.bass_utils import run_bass_kernel_spmd

    a = {k: np.ascontiguousarray(v) for k, v in inputs.items()}
    N, E = a["x"].shape[0], a["src"].shape[0]
    S = E // SUP
    assert S * SUP == E

    w1 = a["L1_gnn_W1"]
    w1_2 = np.zeros((P, P), w1.dtype)
    w1_2[:D, :HID], w1_2[D:2 * D, HID:] = w1, w1
    b1_2 = np.concatenate([a["L1_gnn_b1"], a["L1_gnn_b1"]])[:, None]
    w2 = np.concatenate([a["L1_gnn_W2"], a["L1_gnn_b2"][None]]).reshape(HID + 1, 4, BLK)
    w2_aug = np.zeros((P, WN), w2.dtype)
    w2_aug[:HID + 1] = w2[:, [3, 0, 1, 2]].reshape(HID + 1, WN)
    si_mat = np.zeros((JG, D, JG, D), w1.dtype)
    for j in range(JG):
        si_mat[j, :MUL, j, :MUL] = a["L1_gnn_si_w0"]
        for m in range(3):
            si_mat[j, MUL + m::3, j, MUL + m::3] = a["L1_gnn_si_w1"]

    alpha, c110 = 0.25, 3 ** -0.5
    sel = np.zeros((P, 2, D), np.float32)
    for i in range(2 * MUL):
        for o in range(MUL):
            sel[i * MUL + o, 0, o] = alpha * (c110 if i < MUL else 1.0)
    for c in range(HV + 3 * MUL):
        m, o = divmod(c % (3 * MUL), MUL)
        sel[c, 1, MUL + 3 * o + m] = alpha

    arrays = {
        "x": a["x"],
        "src_t": a["src"].reshape(S, G, P).transpose(0, 2, 1),
        "src_flat": a["src"].reshape(S, 1, SUP),
        "dst_flat": a["dst"],
        "dst_t": a["dst"].reshape(S * G, P).T,
        "ew_t": a["edge_weight"].reshape(S, G, P).transpose(0, 2, 1),
        "sh_t": a["edge_attr_4"].reshape(S, G, P, 4).transpose(0, 2, 1, 3).reshape(S, P, G * 4),
        "ft": a["edge_attr_32"].reshape(S, 2, HALF, D).transpose(0, 1, 3, 2).reshape(S, 2 * D, HALF),
        "w1_2": w1_2, "b1_2": b1_2, "w2_aug": w2_aug, "si_mat": si_mat.reshape(JG * D, JG * D),
        "iota": np.tile(np.arange(WIN, dtype=np.float32), (P, 1)),
        "lane": np.arange(P, dtype=np.float32)[:, None],
        "blocks": np.tile(np.arange(GB, dtype=np.float32) * P, (P, 1)),
        "ident": np.eye(P, dtype=np.float32),
        "sel": sel,
    }
    nc = bacc.Bacc("TRN2", target_bir_lowering=False, num_devices=1)
    sent, args = {}, []
    for name, v in arrays.items():
        v = np.ascontiguousarray(v)
        sent[f"in_{name}"] = v
        args.append(nc.dram_tensor(f"in_{name}", v.shape, mybir.dt.from_np(v.dtype), kind="ExternalInput").ap())
    args.append(nc.dram_tensor("out_0", (N, D), F32, kind="ExternalOutput").ap())
    gnn_two_layers(nc, *args)
    r = run_bass_kernel_spmd(nc, [sent], core_ids=[0])
    return r.results[0]["out_0"]
```
